# Optimizing a Trainium2 kernel written in Bass

```python
import numpy as np
import jax
import jax.numpy as jnp

def _softmax(x, axis=-1):
    return jax.nn.softmax(x, axis=axis)

def _gelu(x):
    return jax.nn.gelu(x, approximate=True)

def _silu(x):
    return jax.nn.silu(x)

def _sigmoid(x):
    return jax.nn.sigmoid(x)

def _layernorm(x, axis=-1, eps=1e-05):
    m = jnp.mean(x, axis=axis, keepdims=True)
    v = jnp.var(x, axis=axis, keepdims=True)
    return (x - m) / jnp.sqrt(v + eps)

def _scatter_add(tgt, idx, src, axis=0):
    return tgt.at[idx].add(src)

def _segment_sum(src, seg, n):
    return jax.ops.segment_sum(src, seg, n)
kernel_name = 'mk_early_fusion_d1_tok_img1024_r4_e1b330'

def setup_inputs(seed: int=0):
    np.random.seed(seed)
    _w = jnp.asarray

    def _rec_inputs():
        import jax
        import jax.numpy as jnp
        _rk = jax.random.key(seed)
        x = -0.000222058 + 0.999998 * jax.random.normal(jax.random.fold_in(_rk, 1), (128, 3, 224, 224), jnp.float32)
        txt = 0.00193382 + 0.183443 * jax.random.normal(jax.random.fold_in(_rk, 2), (128, 77, 256), jnp.float32)
        return (x, txt)
    x, txt = _rec_inputs()

    def _L0_tok_setup():
        import jax, jax.numpy as jnp
        import numpy as np
        P = 16
        C = 3
        D = 256

        def _patchify(x, p):
            B, Cc, H, W = x.shape
            gh, gw = (H // p, W // p)
            x = x.reshape(B, Cc, gh, p, gw, p)
            x = x.transpose(0, 2, 4, 1, 3, 5)
            return x.reshape(B, gh * gw, Cc * p * p)
        key = jax.random.key(seed)
        k1, k2, k3, k4, k5 = jax.random.split(key, 5)
        patch_dim = C * P * P
        s1 = 1.0 / np.sqrt(patch_dim)
        s2 = 1.0 / np.sqrt(D)
        return {'x': jax.random.normal(k1, (32, C, 128, 128), dtype=jnp.float32), 'W1': jax.random.uniform(k2, (patch_dim, D), jnp.float32, -s1, s1), 'b1': jax.random.uniform(k3, (D,), jnp.float32, -s1, s1), 'W2': jax.random.uniform(k4, (D, D), jnp.float32, -s2, s2), 'b2': jax.random.uniform(k5, (D,), jnp.float32, -s2, s2)}
    _L0_tok_all = _L0_tok_setup()
    _L0_tok_in = {k: v for k, v in _L0_tok_all.items() if k in ('W1', 'b1', 'W2', 'b2')}
    del _L0_tok_all

    def _L0_attn_setup():
        import jax, jax.numpy as jnp
        import numpy as np
        DIM = 256
        HEADS = 16
        DIM_HEAD = DIM // HEADS
        LATENT = DIM // 4
        SCALE = DIM_HEAD ** (-0.5)
        key = jax.random.key(seed)
        ks = jax.random.split(key, 8)
        B, S = (2, 512)
        init = lambda k, shape, fan_in: jax.random.normal(k, shape, jnp.float32) * fan_in ** (-0.5)
        return {'x': jax.random.normal(ks[0], (B, S, DIM), jnp.float32), 'Wq': init(ks[1], (DIM, DIM), DIM), 'bq': jnp.zeros((DIM,), jnp.float32), 'Wl': init(ks[2], (DIM, LATENT), DIM), 'bl': jnp.zeros((LATENT,), jnp.float32), 'Wk': init(ks[3], (LATENT, DIM), LATENT), 'bk': jnp.zeros((DIM,), jnp.float32), 'Wv': init(ks[4], (LATENT, DIM), LATENT), 'bv': jnp.zeros((DIM,), jnp.float32), 'Wo': init(ks[5], (DIM, DIM), DIM), 'bo': jnp.zeros((DIM,), jnp.float32)}
    _L0_attn_all = _L0_attn_setup()
    _L0_attn_in = {k: v for k, v in _L0_attn_all.items() if k in ('Wq', 'bq', 'Wl', 'bl', 'Wk', 'bk', 'Wv', 'bv', 'Wo', 'bo')}
    del _L0_attn_all

    def _L0_ffn_setup():
        import jax, jax.numpy as jnp
        import numpy as np
        TOP_K = 2
        key = jax.random.key(seed)
        k1, k2, k3, k4 = jax.random.split(key, 4)
        B_, S, D = (4, 2048, 256)
        E, R = (8, 16)
        x = jax.random.normal(k1, (B_, S, D), dtype=jnp.float32)
        Wg = jax.random.normal(k2, (D, E), dtype=jnp.float32) * 0.02
        A = jax.random.normal(k3, (E, D, R), dtype=jnp.float32) * 0.02
        Bm = jax.random.normal(k4, (E, R, D), dtype=jnp.float32) * 0.02
        return {'x': x, 'Wg': Wg, 'A': A, 'B': Bm}
    _L0_ffn_all = _L0_ffn_setup()
    _L0_ffn_in = {k: v for k, v in _L0_ffn_all.items() if k in ('Wg', 'A', 'B')}
    del _L0_ffn_all
    return {'x': x, 'txt': txt, 'L0_tok_W1': _L0_tok_in['W1'], 'L0_tok_b1': _L0_tok_in['b1'], 'L0_tok_W2': _L0_tok_in['W2'], 'L0_tok_b2': _L0_tok_in['b2'], 'L0_attn_Wq': _L0_attn_in['Wq'], 'L0_attn_bq': _L0_attn_in['bq'], 'L0_attn_Wl': _L0_attn_in['Wl'], 'L0_attn_bl': _L0_attn_in['bl'], 'L0_attn_Wk': _L0_attn_in['Wk'], 'L0_attn_bk': _L0_attn_in['bk'], 'L0_attn_Wv': _L0_attn_in['Wv'], 'L0_attn_bv': _L0_attn_in['bv'], 'L0_attn_Wo': _L0_attn_in['Wo'], 'L0_attn_bo': _L0_attn_in['bo'], 'L0_ffn_Wg': _L0_ffn_in['Wg'], 'L0_ffn_A': _L0_ffn_in['A'], 'L0_ffn_B': _L0_ffn_in['B']}

def reference(x, txt, L0_tok_W1, L0_tok_b1, L0_tok_W2, L0_tok_b2, L0_attn_Wq, L0_attn_bq, L0_attn_Wl, L0_attn_bl, L0_attn_Wk, L0_attn_bk, L0_attn_Wv, L0_attn_bv, L0_attn_Wo, L0_attn_bo, L0_ffn_Wg, L0_ffn_A, L0_ffn_B):
    import jax
    import jax.numpy as jnp

    def _L0_tok_ref(x, W1, b1, W2, b2):
        import jax, jax.numpy as jnp
        import numpy as np
        P = 16
        C = 3
        D = 256

        def _patchify(x, p):
            B, Cc, H, W = x.shape
            gh, gw = (H // p, W // p)
            x = x.reshape(B, Cc, gh, p, gw, p)
            x = x.transpose(0, 2, 4, 1, 3, 5)
            return x.reshape(B, gh * gw, Cc * p * p)
        patches = _patchify(x, P)
        h = jax.nn.silu(jnp.einsum('blk,kd->bld', patches, W1) + b1)
        return jnp.einsum('bld,de->ble', h, W2) + b2

    def _L0_attn_ref(x, Wq, bq, Wl, bl, Wk, bk, Wv, bv, Wo, bo):
        import jax, jax.numpy as jnp
        import numpy as np
        DIM = 256
        HEADS = 16
        DIM_HEAD = DIM // HEADS
        LATENT = DIM // 4
        SCALE = DIM_HEAD ** (-0.5)
        B, S, D = x.shape
        H, Dh = (HEADS, DIM_HEAD)
        q = (x @ Wq + bq).reshape(B, S, H, Dh)
        latent = x @ Wl + bl
        k = (latent @ Wk + bk).reshape(B, S, H, Dh)
        v = (latent @ Wv + bv).reshape(B, S, H, Dh)
        scores = jnp.einsum('bihd,bjhd->bhij', q, k) * SCALE
        attn = jax.nn.softmax(scores, axis=-1)
        out = jnp.einsum('bhij,bjhd->bihd', attn, v).reshape(B, S, D)
        out = out @ Wo + bo
        return out

    def _L0_ffn_ref(x, Wg, A, B):
        import jax, jax.numpy as jnp
        import numpy as np
        TOP_K = 2
        D = x.shape[-1]
        E = Wg.shape[-1]
        xs = x.reshape(-1, D)
        gate_logits = xs @ Wg
        topw, sel = jax.lax.top_k(gate_logits, TOP_K)
        topw = jax.nn.softmax(topw.astype(jnp.float32), axis=-1).astype(x.dtype)
        cw = jnp.sum(jax.nn.one_hot(sel, E, dtype=x.dtype) * topw[..., None], axis=1)
        h = jnp.einsum('td,edr->ter', xs, A)
        hw = h * cw[..., None]
        out = jnp.einsum('ter,erd->td', hw, B)
        return out.reshape(x.shape)
    h = _L0_tok_ref(x, L0_tok_W1, L0_tok_b1, L0_tok_W2, L0_tok_b2)
    h = jnp.concatenate([h, txt], axis=1)
    h = h + _L0_attn_ref(_layernorm(h, axis=-1), L0_attn_Wq, L0_attn_bq, L0_attn_Wl, L0_attn_bl, L0_attn_Wk, L0_attn_bk, L0_attn_Wv, L0_attn_bv, L0_attn_Wo, L0_attn_bo)
    h = h + _L0_ffn_ref(_layernorm(h, axis=-1), L0_ffn_Wg, L0_ffn_A, L0_ffn_B)
    return h

_drawn_inputs = setup_inputs


def setup_inputs(seed=0):
    import zlib

    import numpy as np

    out = dict(_drawn_inputs(seed))
    spreads = {'L0_attn_bq': (0.0, 0.1),
     'L0_attn_bl': (0.0, 0.1),
     'L0_attn_bk': (0.0, 0.1),
     'L0_attn_bv': (0.0, 0.1),
     'L0_attn_bo': (0.0, 0.1)}
    factors = {}
    for name, (base, spread) in spreads.items():
        noise = np.random.default_rng([zlib.crc32(name.encode()), seed]).standard_normal(out[name].shape)
        drawn = base * np.exp(spread * noise) if base else spread * noise
        out[name] = jnp.asarray(drawn.astype(out[name].dtype))
    for name, factor in factors.items():
        out[name] = (out[name] * factor).astype(out[name].dtype)
    return out
```

```python
from contextlib import ExitStack

import concourse.bass as bass
from concourse import mybir

F32 = mybir.dt.float32
BF16 = mybir.dt.bfloat16
I32 = mybir.dt.int32
U32 = mybir.dt.uint32
ALU = mybir.AluOpType
ACT = mybir.ActivationFunctionType
AX_X = mybir.AxisListType.X

IMAGES, CH, SIDE, PATCH = 128, 3, 224, 16
GRID = SIDE // PATCH
PATCHES = GRID * GRID
TXT = 77
TOK = PATCHES + TXT
D = 256
HEADS, HD = 16, 16
LAT = D // 4
EXPERTS, RANK = 8, 16
ER = EXPERTS * RANK
EPS = 1e-5
GROUP = 4
GROUPS = IMAGES // GROUP
ROWS = GROUP * GRID
KT1 = CH * PATCH * PATCH // 128
HALF = GRID // 2
CHUNKS = [(0, 2), (2, 2), (4, 2), (6, 1)]
QT = [98, 98, TXT]
QO = [0, 98, 196]
KEYS = TOK // 3
SLOTS = 6
QPART = [0, 0, 0, 1, 1, 2]
KPART = [0, 1, 2, 0, 1, 0]
SROWS = SLOTS * HD
XROWS = SROWS + 3
VW = 32
CLEARS, SETUP_V = 9, 18
GC = EXPERTS + ER
RSQRT_GUESS = float(0x5F3759DF)
STEPS = HEADS
MA_SLOT, MD_SLOT = 19, 16


def early_fusion(nc, x, txt, eye, W1, b1, W2, b2, Wq, bq, Wl, bl, Wk, bk, Wv, bv, Wo, bo, Wg, A, B, out):
    ctx = ExitStack()

    def sb(name, shape, dt=F32):
        return ctx.enter_context(nc.sbuf_tensor(name, shape, dt))

    def sem(name):
        return ctx.enter_context(nc.semaphore(name))

    with ctx:
        w1 = sb("w1", [128, KT1, D])
        w2 = sb("w2", [128, 2, D])
        wq = sb("wq", [128, 2, D])
        wqp = sb("wqp", [128, 2, 2, HD, 8])
        wo = sb("wo", [128, 2, D])
        wlk = sb("wlk", [128, 2, 2, HD, 8])
        wlv = sb("wlv", [128, 2, D])
        wga = sb("wga", [128, 2, GC])
        wb = sb("wb", [ER, D])
        wl = sb("wl", [128, 2, LAT])
        wlT = sb("wlT", [LAT, 2, 128])
        wk = sb("wk", [LAT, D])
        wkv = sb("wkv", [LAT, 2, D])
        blc = sb("blc", [LAT, 1])
        b1c = sb("b1c", [128, 2])
        bqc = sb("bqc", [128, 2])
        bkc = sb("bkc", [128, 2])
        bvc = sb("bvc", [128, 2])
        bvw = sb("bvw", [128, 2, QT[0]])
        b2r = sb("b2r", [QT[0], D])
        cor = sb("cor", [QT[0], D])
        ident = sb("ident", [128, 128])
        iota_i = sb("iota_i", [QT[0], 3, EXPERTS], I32)
        iota_e = sb("iota_e", [QT[0], 3, EXPERTS])

        raw = sb("raw", [128, CH * PATCH, HALF, PATCH])
        rawp = sb("rawp", [128, 2, CH * PATCH, PATCH])
        xT = sb("xT", [128, KT1, 2, 2, ROWS])
        zring = sb("zring", [128, 2, 2, GRID, GROUP, GRID])
        tnh = sb("tnh", [128, 2, PATCHES])
        h1 = sb("h1", [128, 2, PATCHES])
        hres = sb("hres", [QT[0], 4, 3, D])
        xn1 = sb("xn1", [QT[0], 3, D])
        xn2 = sb("xn2", [QT[0], 3, D])
        xnT1 = sb("xnT1", [128, 2, TOK])
        xnT2 = sb("xnT2", [128, 2, TOK])
        qkf = sb("qkf", [128, 4, TOK])
        qkr = sb("qkr", [128, 4, TOK])
        parts = sb("parts", [128, 3, 4, TOK], BF16)
        qst = sb("qst", [XROWS, 2, HEADS, TOK], BF16)
        kst = sb("kst", [XROWS, 2, HEADS, TOK], BF16)
        mxs = sb("mxs", [KEYS, 2, 3, HEADS])
        msf = sb("msf", [8, TOK])
        msr = sb("msr", [8, TOK])
        msp = sb("msp", [8, 3, TOK], BF16)
        vaug = sb("vaug", [KEYS, 2, 3, HEADS, VW])
        prob = sb("prob", [KEYS, 2, 4, 3, TOK])
        oT = sb("oT", [128, 4, TOK])
        orec = sb("orec", [QT[0], 3, HEADS])
        otok = sb("otok", [QT[0], 3, D])
        otT = sb("otT", [128, 2, TOK])
        st = [sb(f"st{i}", [QT[0], 3, 6]) for i in range(2)]
        mv = [sb(f"mv{i}", [QT[0], 3, 2]) for i in range(2)]
        nw = [sb(f"nw{i}", [QT[0], 4, 3]) for i in range(2)]
        ga = sb("ga", [QT[0], 3, GC])
        gev = sb("gev", [QT[0], 4, 3])
        top = sb("top", [QT[0], 3, 8])
        topi = sb("topi", [QT[0], 3, 8], U32)
        cws = sb("cws", [QT[0], 5, 3, EXPERTS])
        hw = sb("hw", [QT[0], 3, ER])
        hwT = sb("hwT", [ER, TOK])
        ost = sb("ost", [QT[0], 3, D])

        ps_sm = [ctx.enter_context(nc.psum_tensor(f"ps_sm{i}", [128, 512], F32)) for i in range(2)]
        ps_st = [ctx.enter_context(nc.psum_tensor(f"ps_st{i}", [128, 512], F32)) for i in range(2)]
        ps_po = ctx.enter_context(nc.psum_tensor("ps_po", [128, 512], F32))
        ps_ma = [ctx.enter_context(nc.psum_tensor(f"ps_ma{i}", [128, 512], F32)) for i in range(2)]
        ps_md = [ctx.enter_context(nc.psum_tensor("ps_md", [128, 512], F32))]

        sm_full, sm_free = sem("sm_full"), sem("sm_free")
        st_full, exp_done = sem("st_full"), sem("exp_done")
        po_full, po_free = sem("po_full"), sem("po_free")
        ma_full, ma_free = sem("ma_full"), sem("ma_free")
        md_full, md_free = sem("md_full"), sem("md_free")
        w_in, b_in = sem("w_in"), sem("b_in")
        raw_in = sem("raw_in")
        rawp_done = sem("rawp_done")
        rawp_read = sem("rawp_read")
        raw_clear = sem("raw_clear")
        txt_in = sem("txt_in")
        stack_in = [sem(f"stack_in{i}") for i in range(4)]
        mrow_in = [sem(f"mrow_in{i}") for i in range(4)]
        store = sem("store")
        tanh_done, h1_done = sem("tanh_done"), sem("h1_done")
        stat = [sem("stat1"), sem("stat2")]
        newton = [sem("newton1"), sem("newton2")]
        rstd = [sem("rstd1"), sem("rstd2")]
        xn_done = [sem("xn1_done"), sem("xn2_done")]
        const_added = sem("const_added")
        hi_done, mid_done = sem("hi_done"), sem("mid_done")
        res_done, lo_done = sem("res_done"), sem("lo_done")
        mhi_done, mchain, msplit = sem("mhi_done"), sem("mchain"), sem("msplit")
        orec_done = sem("orec_done")
        top_done = sem("top_done")
        gexp_done = sem("gexp_done")
        gden_done = sem("gden_done")
        mask_done = sem("mask_done")
        gchain, cw_done = sem("gchain"), sem("cw_done")
        hw_done = sem("hw_done")
        passed = sem("passed")
        cleared, setup_pe, setup_v, setup_g = sem("cleared"), sem("setup_pe"), sem("setup_v"), sem("setup_g")

        class Linear:

            def __init__(self, turn, a, b):
                self.turn, self.a, self.b = turn, a, b

            def __add__(self, n):
                return Linear(self.turn, self.a, self.b + n)

            def __sub__(self, n):
                return Linear(self.turn, self.a, self.b - n)

            def __mul__(self, n):
                return Linear(self.turn, self.a * n, self.b * n)

            __radd__, __rmul__ = __add__, __mul__

            def value(self):
                return self.turn * self.a + self.b

        def count(v):
            return v.value() if isinstance(v, Linear) else v

        def due(v):
            return isinstance(v, Linear) or v > 0


        class Units:

            def __init__(self, banks, per_slot):
                self.banks, self.per_turn, self.count, self.g, self.start = banks, GROUP * per_slot, 0, None, 0

            def enter(self, g):
                assert self.per_turn % self.banks == 0
                self.g, self.start = g, self.count

            def leave(self, turns):
                assert self.count - self.start == self.per_turn, (self.count - self.start, self.per_turn)
                self.count, self.g = self.start + turns * self.per_turn, None

            def so_far(self, ahead=0):
                n = self.count + ahead
                return n if self.g is None else Linear(self.g, self.per_turn, n)

            def next(self):
                self.count += 1
                return (self.count - 1) % self.banks, self.so_far()

        class Slot:

            def __init__(self, g, s, tok=True):
                self.g, self.s, self.tok = g, s, tok

            def image(self, k):
                return self.g * GROUP + (2 + self.s + k)

            def place(self, k):
                return count(self.image(k))

            def mod(self, k, m):
                return (2 + self.s + k) % m

            def has(self, k):
                i = self.image(k)
                return not isinstance(i, int) or 0 <= i < IMAGES

            def group(self):
                return self.g + 2

            def landed(self, k, each):
                return (self.g * 2 + ((2 + self.s + k) // 2 + 1)) * each

        TURNS = GROUPS - 2
        HEAD = [Slot(-2, s) for s in range(4)]
        FILL = [Slot(-1, s) for s in range(4)]
        DRAIN = [Slot(TURNS, s, tok=False) for s in range(4)] + [Slot(TURNS + 1, s, tok=False) for s in range(3)]

        def drive(eng, slot, tok_only, counters):
            for p in HEAD:
                tok_only(p)
            for p in FILL:
                slot(p)
            with eng.Fori(0, TURNS) as g:
                for c in counters:
                    c.enter(g)
                for s in range(4):
                    copy = eng.alloc_register(f"turn{s}")
                    eng.reg_mov(copy, g)
                    turn = eng.snap(copy, min_val=0, max_val=TURNS - 1)
                    for c in counters:
                        c.g = turn
                    slot(Slot(Linear(turn, 1, 0), s))
            for c in counters:
                c.leave(TURNS)
            for p in DRAIN:
                slot(p)

        STACK, MROW, RAW = 12 * 16, 3 * 16, 24 * 16
        block = ctx.enter_context(nc.Block())

        x_v = x.rearrange("b c (gh ph) w -> b gh c ph w", ph=PATCH)
        out_v = out[:, 0:PATCHES, :].rearrange("b (gh gw) d -> b gw gh d", gw=GRID)

        @block.sync
        def _(sp):
            md = Units(1, MD_SLOT)

            def load_raw(group):
                first = group * GROUP if isinstance(group, int) else count(group) % GROUPS * GROUP
                for half in range(2):
                    for b in range(GROUP):
                        for c in range(CH):
                            row = 64 * half + b * GRID
                            sp.dma_start(raw[row:row + GRID, c * PATCH:(c + 1) * PATCH, :, :]
                                         .rearrange("p r w q -> p r (w q)"),
                                         x_v[first + b, :, c, :,
                                             half * HALF * PATCH:(half + 1) * HALF * PATCH]).then_inc(raw_in, 16)

            sp.wait_ge(raw_clear, 1)
            load_raw(0)
            sp.dma_start(ident[:], eye).then_inc(w_in, 16)
            for dst, src in ((w1, W1), (w2, W2), (wq, Wq), (wo, Wo), (wl, Wl)):
                sp.dma_start(dst[:], src.rearrange("(k p) n -> p k n", p=128)).then_inc(w_in, 16)
            sp.dma_start(wk[:], Wk).then_inc(w_in, 16)
            sp.dma_start(wkv[:, 1, :], Wv).then_inc(w_in, 16)
            sp.dma_start(wga[:, :, 0:EXPERTS], Wg.rearrange("(k p) e -> p k e", p=128)).then_inc(w_in, 16)
            for k in range(2):
                sp.dma_start(wga[:, k, EXPERTS:GC].rearrange("p (e r) -> p e r", e=EXPERTS),
                             A[:, k * 128:(k + 1) * 128, :].rearrange("e p r -> p e r")).then_inc(w_in, 16)
            sp.dma_start(wb[:], B.rearrange("e r d -> (e r) d")).then_inc(w_in, 16)
            sp.dma_start(blc[:], bl.rearrange("(p a) -> p a", a=1)).then_inc(b_in, 16)
            for dst, src in ((b1c, b1), (bvc, bv)):
                for k in range(2):
                    sp.dma_start(dst[:, k:k + 1], src[k * 128:(k + 1) * 128].rearrange("(p a) -> p a", a=1)) \
                      .then_inc(b_in, 16)
            for dst, src in ((bqc, bq), (bkc, bk)):
                for k in range(2):
                    sp.dma_start(dst[:, k:k + 1], src[k * 128:(k + 1) * 128].rearrange("(h d) -> d h", h=8),
                                 allow_slow_non_contiguous=True) \
                      .then_inc(b_in, 16)
            sp.dma_start(b2r[:], b2.rearrange("(a d) -> a d", a=1).broadcast_to([QT[0], D])).then_inc(b_in, 16)
            sp.dma_start(cor[:], bo.rearrange("(a d) -> a d", a=1).broadcast_to([QT[0], D])).then_inc(b_in, 16)
            sp.wait_ge(cleared, CLEARS)

            def reload(p):
                if p.tok and p.s == 3:
                    sp.wait_ge(rawp_done, count(4 * p.group() + 4))
                    sp.sem_inc(passed, 1)
                    load_raw(p.group() + 1)

            def text(p):
                if p.has(2):
                    if p.has(-2):
                        sp.wait_ge(md_free, count(md.so_far()))
                    sp.sem_inc(passed, 1)
                    sp.dma_start(hres[0:TXT, p.mod(2, 4), 2, :], txt[p.place(2), :, :]).then_inc(txt_in, 16)

            def max_rows(p, k, half):
                if p.has(k):
                    sp.wait_ge(msplit, count(2 * p.image(k) + half + 1))
                    sp.sem_inc(passed, 1)
                    if due(48 * p.image(k - 2) + 24 * half + 24):
                        sp.wait_ge(st_full, count(48 * p.image(k - 2) + 24 * half + 24))
                    sp.sem_inc(passed, 1)
                    y = p.mod(k, 2)
                    for r in range(3):
                        sp.dma_start(qst[SROWS + r:SROWS + r + 1, y, 8 * half:8 * half + 8, :], msp[:, r, :]) \
                          .then_inc(mrow_in[2 * y + half], 16)

            def stack(p, half):
                if p.has(2):
                    sp.wait_ge(hi_done, count(4 * p.image(2) + 4))
                    sp.wait_ge(mid_done, count(4 * p.image(2) + 4))
                    sp.wait_ge(lo_done, count(4 * p.image(2) + 4))
                    sp.sem_inc(passed, 1)
                    if due(48 * p.image(0) + 24 * half + 24):
                        sp.wait_ge(st_full, count(48 * p.image(0) + 24 * half + 24))
                    sp.sem_inc(passed, 1)
                    y = p.mod(2, 2)
                    for dst, t, which in ((qst, 0, QPART), (kst, 2, KPART)):
                        for row, part in enumerate(which):
                            sp.dma_start(dst[row * HD:(row + 1) * HD, y, 8 * half:8 * half + 8, :],
                                         parts[:, part, t + half, :]).then_inc(stack_in[2 * y + half], 16)

            def save(p):
                if p.has(-1):
                    i = p.place(-1)
                    sp.wait_ge(md_free, count(md.so_far()))
                    sp.sem_inc(passed, 1)
                    for t in range(2):
                        sp.dma_start(out_v[i, t * HALF:(t + 1) * HALF, :, :], ost[0:QT[t], t, :]).then_inc(store, 16)
                    sp.dma_start(out[i, PATCHES:TOK, :], ost[0:TXT, 2, :]).then_inc(store, 16)

            def count_units(p):
                md.count += 1 * p.has(0) + 12 * p.has(-1) + 2 * p.has(2) + 1 * p.has(1)

            def slot(p):
                max_rows(p, 0, 1)
                text(p)
                reload(p)
                max_rows(p, 1, 0)
                stack(p, 0)
                count_units(p)
                stack(p, 1)
                save(p)

            drive(sp, slot, reload, [md])
            sp.wait_ge(raw_in, (GROUPS + 1) * RAW)
            sp.wait_ge(store, 3 * 16 * IMAGES)

        @block.tensor
        def _(pe):
            ma, md = Units(2, MA_SLOT), Units(1, MD_SLOT)

            pe.wait_ge(w_in, 16 * 12)
            pe.wait_ge(b_in, 16 * 11)
            for k in range(2):
                last = nc.tensor.transpose(ps_md[0][0:LAT, k * 128:(k + 1) * 128], wl[:, k, :], ident[:])
            last.then_inc(setup_pe, 1)
            pe.wait_ge(setup_v, 3)
            for k in range(2):
                nc.tensor.matmul(ps_sm[k][:, :], wlT[:, k, :], wkv[:, :, :].rearrange("p a n -> p (a n)"),
                                 start=True, stop=True)
            for a in range(2):
                for k in range(2):
                    last = nc.tensor.matmul(ps_st[a][:, k:k + 1], wkv[:, a, k * 128:(k + 1) * 128], blc[:],
                                            start=(k == 0), stop=True, skip_group_check=True)
            last.then_inc(setup_pe, 1)
            pe.wait_ge(setup_v, 14)
            for k in range(2):
                last = nc.tensor.matmul(ps_md[0][0:QT[0], 0:D], bvw[:, k, :], wo[:, k, :],
                                        start=(k == 0), stop=(k == 1))
            last.then_inc(setup_pe, 1)
            pe.wait_ge(setup_v, SETUP_V)
            pe.wait_ge(cleared, CLEARS)

            def ma_unit():
                bank, n = ma.next()
                if due(ma.so_far(-2)):
                    pe.wait_ge(ma_free, count(ma.so_far(-2)))
                return ps_ma[bank]

            def md_unit():
                bank, n = md.next()
                if due(md.so_far(-1)):
                    pe.wait_ge(md_free, count(md.so_far(-1)))
                return ps_md[bank]

            def tok_transpose(p):
                if p.tok:
                    cols = CHUNKS[p.s][1]
                    pe.wait_ge(rawp_done, count(4 * p.group() + p.s + 1))
                    for u in range(KT1 // 2):
                        bank = ma_unit()
                        pe.sem_inc(passed, 1)
                        for j in range(2):
                            k = 2 * u + j
                            for w in range(cols):
                                a = (j * cols + w) * 128
                                last = nc.tensor.transpose(bank[:, a:a + 128],
                                                           rawp[:, w, 8 * k:8 * k + 8, :]
                                                           .rearrange("p r q -> p (r q)"), ident[:])
                        last.then_inc(ma_full, 1)

            def tok_layer1(p, m, ready):
                if p.tok:
                    n = 2 * CHUNKS[p.s][1] * ROWS
                    pe.wait_ge(ma_free, count(ready))
                    bank = ma_unit()
                    for k in range(KT1):
                        last = nc.tensor.matmul(bank[:, 0:n], w1[:, k, m * 128:(m + 1) * 128],
                                                xT[:, k, 0:n // (2 * ROWS), :, :].rearrange("p w a n -> p (w a n)"),
                                                start=(k == 0), stop=(k == KT1 - 1))
                        if m == 0 and k == 0:
                            last.then_inc(rawp_read, 1)
                    last.then_inc(ma_full, 1)

            def layer2(p):
                if p.has(2):
                    pe.wait_ge(h1_done, count(p.image(2) + 1))
                    for t in range(2):
                        bank = md_unit()
                        for k in range(2):
                            last = nc.tensor.matmul(bank[0:QT[t], 0:D], h1[:, k, QO[t]:QO[t] + QT[t]], w2[:, k, :],
                                                    start=(k == 0), stop=(k == 1))
                        last.then_inc(md_full, 1)

            def feature_major(src):
                for f in range(2):
                    bank = ma_unit()
                    for t in range(3):
                        last = nc.tensor.transpose(bank[:, QO[t]:QO[t] + QT[t]],
                                                   src[0:QT[t], t, f * 128:(f + 1) * 128], ident[0:QT[t], 0:QT[t]])
                    last.then_inc(ma_full, 1)

            def xn_transpose(p, k, ln, src):
                if p.has(k):
                    pe.wait_ge(xn_done[ln], count(3 * p.image(k) + 3))
                    feature_major(src)

            def project(p, w):
                if p.has(2):
                    pe.wait_ge(ma_free, count(ma.so_far()))
                    for m in range(2):
                        bank = ma_unit()
                        for k in range(2):
                            last = nc.tensor.matmul(bank[:, 0:TOK], w[:, k, m, :, :].rearrange("p d h -> p (d h)"),
                                                    xnT1[:, k, :],
                                                    start=(k == 0), stop=(k == 1))
                        last.then_inc(ma_full, 1)

            def values(p):
                if p.has(1):
                    for t in range(3):
                        bank = ma_unit()
                        for k in range(2):
                            last = nc.tensor.matmul(bank[0:KEYS, 0:D], xnT1[:, k, t * KEYS:(t + 1) * KEYS],
                                                    wlv[:, k, :], start=(k == 0), stop=(k == 1))
                        last.then_inc(ma_full, 1)

            def max_scores(p, h, t):
                if p.has(1):
                    y = p.mod(1, 2)
                    if h % 8 == 0 and t == 0:
                        pe.wait_ge(stack_in[2 * y + h // 8], count(p.landed(1, STACK)))
                    bank = (3 * h + t) % 2
                    if due(48 * p.image(1) + 3 * h + t - 1):
                        pe.wait_ge(sm_free, count(48 * p.image(1) + 3 * h + t - 1))
                    nc.tensor.matmul(ps_sm[bank][0:KEYS, 0:TOK], qst[0:SROWS, y, h, t * KEYS:(t + 1) * KEYS],
                                     kst[0:SROWS, y, h, :], start=True, stop=True).then_inc(sm_full, 1)

            def key_scores(p, h, t):
                if p.has(0):
                    y = p.mod(0, 2)
                    if h % 8 == 0 and t == 0:
                        pe.wait_ge(mrow_in[2 * y + h // 8], count(p.landed(0, MROW)))
                    bank = (3 * h + t) % 2
                    if due(48 * p.image(0) + 3 * h + t - 1):
                        pe.wait_ge(exp_done, count(48 * p.image(0) + 3 * h + t - 1))
                    nc.tensor.matmul(ps_st[bank][0:KEYS, 0:TOK], kst[:, y, h, t * KEYS:(t + 1) * KEYS],
                                     qst[:, y, h, :], start=True, stop=True).then_inc(st_full, 1)

            def max_transpose(p, k, half):
                if p.has(k):
                    pe.wait_ge(sm_free, count(48 * p.image(k) + 24 * half + 24))
                    bank = md_unit()
                    for t in range(3):
                        last = nc.tensor.transpose(bank[0:8, t * KEYS:(t + 1) * KEYS],
                                                   mxs[:, p.mod(k, 2), t, 8 * half:8 * half + 8],
                                                   ident[0:KEYS, 0:KEYS])
                    last.then_inc(md_full, 1)

            def weigh(p, k, g):
                if p.has(k):
                    i, y = p.image(k), p.mod(k, 2)
                    pe.wait_ge(exp_done, count(48 * i + 12 * g + 12))
                    if due(4 * i + g):
                        pe.wait_ge(po_free, count(4 * i + g))
                    for t in range(3):
                        for j in range(4):
                            last = nc.tensor.matmul(ps_po[VW * j:VW * (j + 1), 0:TOK], vaug[:, y, t, 4 * g + j, :],
                                                    prob[:, g % 2, j, t, :], start=(t == 0), stop=(t == 2))
                    last.then_inc(po_full, 1)

            def out_transpose(p):
                if p.has(-1):
                    pe.wait_ge(po_free, count(4 * p.image(-1) + 4))
                    for t in range(3):
                        bank = md_unit()
                        for g in range(4):
                            last = nc.tensor.transpose(bank[0:QT[t], g * 128:(g + 1) * 128],
                                                       oT[:, g, QO[t]:QO[t] + QT[t]], ident[:])
                        last.then_inc(md_full, 1)

            def otok_transpose(p, ready):
                if p.has(-1):
                    pe.wait_ge(md_free, count(ready))
                    feature_major(otok)

            def out_project(p):
                if p.has(-1):
                    pe.wait_ge(ma_free, count(ma.so_far()))
                    for t in range(3):
                        bank = md_unit()
                        for k in range(2):
                            last = nc.tensor.matmul(bank[0:QT[t], 0:D], otT[:, k, QO[t]:QO[t] + QT[t]], wo[:, k, :],
                                                    start=(k == 0), stop=(k == 1))
                        last.then_inc(md_full, 1)

            def expert_in(p, ready):
                if p.has(-1):
                    pe.wait_ge(ma_free, count(ready))
                    for t in range(3):
                        bank = md_unit()
                        for k in range(2):
                            last = nc.tensor.matmul(bank[0:QT[t], 0:GC], xnT2[:, k, QO[t]:QO[t] + QT[t]],
                                                    wga[:, k, :], start=(k == 0), stop=(k == 1))
                        last.then_inc(md_full, 1)

            def expert_transpose(p):
                if p.has(-1):
                    pe.wait_ge(hw_done, count(p.image(-1) + 1))
                    bank = ma_unit()
                    for t in range(3):
                        last = nc.tensor.transpose(bank[:, QO[t]:QO[t] + QT[t]], hw[0:QT[t], t, :],
                                                   ident[0:QT[t], 0:QT[t]])
                    last.then_inc(ma_full, 1)

            def expert_out(p):
                if p.has(-1):
                    pe.wait_ge(ma_free, count(ma.so_far()))
                    for t in range(3):
                        bank = md_unit()
                        nc.tensor.matmul(bank[0:QT[t], 0:D], hwT[:, QO[t]:QO[t] + QT[t]], wb[:],
                                         start=True, stop=True).then_inc(md_full, 1)

            def slot(p):
                for h in range(STEPS):
                    for t in range(2):
                        max_scores(p, h, t)
                        key_scores(p, h, t)
                    if h == 1:
                        weigh(p, -1, 3)
                        max_transpose(p, 0, 1)
                    if h == 2:
                        values(p)
                        out_transpose(p)
                        otok_ready = md.so_far()
                    if h == 3:
                        layer2(p)
                        tok_transpose(p)
                        xT_ready = ma.so_far()
                    if h == 4:
                        otok_transpose(p, otok_ready)
                    if h == 5:
                        weigh(p, 0, 0)
                        out_project(p)
                    if h == 7:
                        xn_transpose(p, 2, 0, xn1)
                    if h == 8:
                        project(p, wqp)
                        xn_transpose(p, -1, 1, xn2)
                        xnT2_ready = ma.so_far()
                    if h == 9:
                        weigh(p, 0, 1)
                        project(p, wlk)
                        max_transpose(p, 1, 0)
                        expert_in(p, xnT2_ready)
                    if h == 12:
                        tok_layer1(p, 0, xT_ready)
                    if h == 13:
                        weigh(p, 0, 2)
                    if h == 14:
                        tok_layer1(p, 1, xT_ready)
                        expert_transpose(p)
                    if h == 15:
                        expert_out(p)
                    max_scores(p, h, 2)
                    key_scores(p, h, 2)

            def tok_only(p):
                tok_transpose(p)
                ready = ma.so_far()
                tok_layer1(p, 0, ready)
                tok_layer1(p, 1, ready)

            drive(pe, slot, tok_only, [ma, md])

        @block.scalar
        def _(act):
            ma = Units(2, MA_SLOT)

            def ma_unit():
                bank, n = ma.next()
                act.wait_ge(ma_full, count(n))
                return ps_ma[bank]

            act.wait_ge(setup_v, SETUP_V)
            act.wait_ge(cleared, CLEARS)

            def tok_evac(p):
                if p.tok:
                    cols = CHUNKS[p.s][1]
                    for u in range(KT1 // 2):
                        bank = ma_unit()
                        nc.scalar.activation(xT[:, 2 * u:2 * u + 2, 0:cols, :, :].rearrange("p j w a n -> p (j w) a n"),
                                             bank[:, 0:2 * cols * 128].rearrange("p (t a n) -> p t a n", a=2, n=64)
                                             [:, :, :, 0:ROWS], ACT.Copy).then_inc(ma_free, 1)

            def z_evac(p, m):
                if p.tok:
                    col, cols = CHUNKS[p.s]
                    if m == 0 and p.s == 0:
                        if due((p.group() - 1) * GROUP):
                            act.wait_ge(h1_done, count((p.group() - 1) * GROUP))
                    bank = ma_unit()
                    nc.scalar.activation(zring[:, count(p.group()) % 2, m, :, :, :].rearrange("p (a w) b g -> p w a (b g)", a=2)
                                         [:, col:col + cols, :, :],
                                         bank[:, 0:2 * cols * ROWS].rearrange("p (w a n) -> p w a n", a=2, w=cols),
                                         ACT.Identity, bias=b1c[:, m:m + 1]).then_inc(ma_free, 1)

            def tanh(p):
                if p.has(2):
                    act.wait_ge(ma_free, count(ma.so_far()))
                    if due(p.image(1) + 1):
                        act.wait_ge(h1_done, count(p.image(1) + 1))
                    z = zring[:, count(p.group() - 1) % 2, :, :, p.s, :]
                    nc.scalar.activation(tnh[:].rearrange("p m (w g) -> p m w g", w=GRID), z, ACT.Tanh,
                                         scale=0.5).then_inc(tanh_done, 1)

            def value_evac(p):
                if p.has(1):
                    for t in range(3):
                        bank = ma_unit()
                        nc.scalar.activation(vaug[:, p.mod(1, 2), t, :, 0:HD],
                                             bank[0:KEYS, 0:D].rearrange("p (h d) -> p h d", h=HEADS),
                                             ACT.Copy).then_inc(ma_free, 1)

            def feature_evac(p, k, dst):
                if p.has(k):
                    for f in range(2):
                        bank = ma_unit()
                        nc.scalar.activation(dst[:, f, :], bank[:, 0:TOK], ACT.Copy).then_inc(ma_free, 1)

            def qk_evac(p, a, bias):
                if p.has(2):
                    i = p.image(2)
                    if a == 0:
                        if due(4 * i):
                            act.wait_ge(res_done, count(4 * i))
                        if due(4 * i):
                            act.wait_ge(lo_done, count(4 * i))
                        if not (isinstance(i, int) and i == 0):
                            for half in range(2):
                                act.wait_ge(stack_in[2 * p.mod(1, 2) + half], count(p.landed(1, STACK)))
                    for m in range(2):
                        bank = ma_unit()
                        nc.scalar.activation(qkf[:, a + m, :], bank[:, 0:TOK], ACT.Identity,
                                             bias=bias[:, m:m + 1]).then_inc(ma_free, 1)
                    for m in range(2):
                        act.wait_ge(ma_free, count(ma.so_far(m - 1)))
                        nc.scalar.activation(parts[:, 0, a + m, :], qkf[:, a + m, :], ACT.Copy).then_inc(hi_done, 1)

            def expscore(p, h, t):
                if p.has(0):
                    i, g = p.image(0), h // 4
                    if h % 4 == 0 and t == 0:
                        if due(4 * i + g - 1):
                            act.wait_ge(po_full, count(4 * i + g - 1))
                    act.wait_ge(st_full, count(48 * i + 3 * h + t + 1))
                    nc.scalar.activation(prob[:, g % 2, h % 4, t, :], ps_st[(3 * h + t) % 2][0:KEYS, 0:TOK], ACT.Exp,
                                         scale=HD ** -0.5).then_inc(exp_done, 1)

            def out_evac(p, k, g):
                if p.has(k):
                    if g == 0:
                        pass
                    act.wait_ge(po_full, count(4 * p.image(k) + g + 1))
                    nc.scalar.activation(oT[:, g, :], ps_po[:, 0:TOK], ACT.Copy).then_inc(po_free, 1)

            def gate_exp(p):
                if p.has(-1):
                    i = p.image(-1)
                    act.wait_ge(top_done, count(7 * i + 4))
                    if due(i):
                        act.wait_ge(cw_done, count(i))
                    nc.scalar.activation(gev[:, 1, :], gev[:, 0, :], ACT.Exp).then_inc(gexp_done, 1)

            def expert_evac(p):
                if p.has(-1):
                    bank = ma_unit()
                    nc.scalar.activation(hwT[:, :], bank[:, 0:TOK], ACT.Copy).then_inc(ma_free, 1)

            def slot(p):
                for h in range(STEPS):
                    expscore(p, h, 0)
                    expscore(p, h, 1)
                    if h == 0:
                        tanh(p)
                    if h == 1:
                        out_evac(p, -1, 3)
                    if h == 2:
                        value_evac(p)
                    if h == 3:
                        tok_evac(p)
                    if h == 4:
                        feature_evac(p, -1, otT)
                    if h == 5:
                        out_evac(p, 0, 0)
                    if h == 7:
                        feature_evac(p, 2, xnT1)
                    if h == 8:
                        qk_evac(p, 0, bqc)
                        feature_evac(p, -1, xnT2)
                    if h == 9:
                        out_evac(p, 0, 1)
                        qk_evac(p, 2, bkc)
                    if h == 11:
                        gate_exp(p)
                    if h == 12:
                        z_evac(p, 0)
                    if h == 13:
                        out_evac(p, 0, 2)
                    if h == 14:
                        z_evac(p, 1)
                        expert_evac(p)
                    expscore(p, h, 2)

            def tok_only(p):
                tok_evac(p)
                z_evac(p, 0)
                z_evac(p, 1)

            drive(act, slot, tok_only, [ma])

        @block.vector
        def _(dve):
            md = Units(1, MD_SLOT)

            def md_unit():
                bank, n = md.next()
                dve.wait_ge(md_full, count(n))
                return ps_md[bank]

            nc.vector.memset(raw[:], 0.0).then_inc(raw_clear, 1)
            for c in range(2):
                nc.vector.memset(mv[c][:], 0.0).then_inc(cleared, 1)
            nc.vector.memset(hres[:], 0.0).then_inc(cleared, 1)
            nc.vector.memset(ga[:], 0.0).then_inc(cleared, 1)
            nc.vector.memset(top[:], 0.0).then_inc(cleared, 1)
            nc.vector.memset(topi[:], 0).then_inc(cleared, 1)
            nc.vector.memset(vaug[:], 0.0).then_inc(cleared, 1)
            nc.vector.memset(kst[SROWS:XROWS, :, :, :], 1.0).then_inc(cleared, 1)
            dve.wait_ge(cleared, CLEARS - 1)
            nc.vector.memset(vaug[:, :, :, :, HD:HD + 1], 1.0).then_inc(cleared, 1)

            dve.wait_ge(w_in, 16 * 12)
            for m in range(2):
                nc.vector.tensor_copy(wkv[:, 0, m * 128:(m + 1) * 128].rearrange("p (d h) -> p d h", h=8),
                                      wk[:, m * 128:(m + 1) * 128].rearrange("p (h d) -> p d h", h=8)) \
                  .then_inc(setup_v, 1)
            dve.wait_ge(setup_pe, 1)
            nc.vector.tensor_copy(wlT[:], ps_md[0][0:LAT, 0:256].rearrange("p (k n) -> p k n", k=2)).then_inc(setup_v, 1)
            dve.wait_ge(setup_pe, 2)
            dve.wait_ge(b_in, 16 * 11)
            for k in range(2):
                nc.vector.tensor_copy(wlk[:, k, :, :, :].rearrange("p m d h -> p (m d h)"), ps_sm[k][:, 0:D]) \
                  .then_inc(setup_v, 1)
                for m in range(2):
                    nc.vector.tensor_copy(wqp[:, k, m, :, :], wq[:, k, m * 128:(m + 1) * 128]
                                          .rearrange("p (h d) -> p d h", h=8)).then_inc(setup_v, 1)
                nc.vector.tensor_copy(wlv[:, k, :], ps_sm[k][:, D:2 * D]).then_inc(setup_v, 1)
            nc.vector.tensor_tensor(bvc[:], bvc[:], ps_st[1][:, 0:2], ALU.add).then_inc(setup_v, 1)
            dve.wait_ge(setup_v, 12)
            for k in range(2):
                nc.vector.tensor_copy(bvw[:, k, :], bvc[:, k:k + 1].broadcast_to([128, QT[0]])).then_inc(setup_v, 1)
            nc.vector.tensor_tensor(bkc[:], bkc[:], ps_st[0][:, 0:2], ALU.add).then_inc(setup_v, 1)
            nc.vector.tensor_scalar(w2[:], w2[:], 0.5, None, ALU.mult).then_inc(setup_v, 1)
            dve.wait_ge(setup_g, 1)
            nc.vector.tensor_copy(iota_e[:], iota_i[:]).then_inc(setup_v, 1)
            dve.wait_ge(setup_pe, 3)
            nc.vector.tensor_tensor(cor[:], cor[:], ps_md[0][0:QT[0], 0:D], ALU.add).then_inc(setup_v, 1)

            def product(p):
                if p.has(2):
                    dve.wait_ge(tanh_done, count(p.image(2) + 1))
                    z = zring[:, count(p.group() - 1) % 2, :, :, p.s, :].rearrange("p m w g -> p (m w) g")
                    nc.vector.scalar_tensor_tensor(h1[:].rearrange("p m (w g) -> p (m w) g", w=GRID),
                                                   tnh[:].rearrange("p m (w g) -> p (m w) g", w=GRID), 1.0, z,
                                                   ALU.add, ALU.mult).then_inc(h1_done, 1)

            def reduce_max(p, h, t):
                if p.has(1):
                    dve.wait_ge(sm_full, count(48 * p.image(1) + 3 * h + t + 1))
                    nc.vector.tensor_reduce(mxs[:, p.mod(1, 2), t, h:h + 1], ps_sm[(3 * h + t) % 2][0:KEYS, 0:TOK],
                                            AX_X, ALU.max, negate=True).then_inc(sm_free, 1)

            def max_evac(p, k, half):
                if p.has(k):
                    u = 2 * p.image(k) + half
                    if due(u):
                        dve.wait_ge(msplit, count(u))
                    bank = md_unit()
                    nc.vector.tensor_copy(msf[:], bank[0:8, 0:TOK]).then_inc(md_free, 1)
                    dve.wait_ge(md_free, count(md.so_far()))
                    if not (isinstance(u, int) and u == 0):
                        kk, hh = (k, 0) if half else (k - 1, 1)
                        dve.wait_ge(mrow_in[2 * p.mod(kk, 2) + hh], count(p.landed(kk, MROW)))
                    nc.vector.tensor_copy(msp[:, 0, :], msf[:]).then_inc(mhi_done, 1)

            def normalise(p):
                if p.has(-1):
                    for t in range(3):
                        bank = md_unit()
                        v = bank[0:QT[t], :].rearrange("p (h w) -> p h w", h=HEADS)
                        nc.vector.reciprocal(orec[0:QT[t], t, :], v[:, :, HD:HD + 1].rearrange("p h w -> p (h w)")) \
                          .then_inc(orec_done, 1)
                        dve.wait_ge(orec_done, count(3 * p.image(-1) + t + 1))
                        nc.vector.tensor_tensor(otok[0:QT[t], t, :].rearrange("p (h d) -> p h d", h=HEADS),
                                                v[:, :, 0:HD],
                                                orec[0:QT[t], t, :].unsqueeze(2).broadcast_to([QT[t], HEADS, HD]),
                                                ALU.mult).then_inc(md_free, 1)

            def statistics(i, ln, ring):
                for t in range(3):
                    nc.vector.bn_stats(st[ln][0:QT[t], t, :], hres[0:QT[t], ring, t, :]).then_inc(stat[ln], 1)
                for t in range(3):
                    dve.wait_ge(stat[ln], count(6 * i + t + 1))
                    dve.sem_inc(passed, 1)
                    nc.vector.bn_aggr(mv[ln][0:QT[t], t, :], st[ln][0:QT[t], t, :]).then_inc(stat[ln], 1)

            def layer2_evac(p):
                if p.has(2):
                    i, ring = p.image(2), p.mod(2, 4)
                    for t in range(2):
                        bank = md_unit()
                        nc.vector.tensor_tensor(hres[0:QT[t], ring, t, :], bank[0:QT[t], 0:D], b2r[0:QT[t], :],
                                                ALU.add).then_inc(md_free, 1)
                    dve.wait_ge(txt_in, count(16 * i + 16))
                    dve.wait_ge(md_free, count(md.so_far()))
                    statistics(i, 0, ring)

            def residual(p):
                if p.has(-1):
                    i, ring = p.image(-1), p.mod(-1, 4)
                    dve.wait_ge(const_added, count(i + 1))
                    for t in range(3):
                        bank = md_unit()
                        r = hres[0:QT[t], ring, t, :]
                        nc.vector.tensor_tensor(r, bank[0:QT[t], 0:D], r, ALU.add).then_inc(md_free, 1)
                    dve.wait_ge(md_free, count(md.so_far()))
                    statistics(i, 1, ring)

            def apply(p, k, ln, dst):
                if p.has(k):
                    i, ring = p.image(k), p.mod(k, 4)
                    dve.wait_ge(rstd[ln], count(i + 1))
                    for t in range(3):
                        nc.vector.tensor_scalar(dst[0:QT[t], t, :], hres[0:QT[t], ring, t, :],
                                                mv[ln][0:QT[t], t, 0:1], nw[ln][0:QT[t], 1, t:t + 1],
                                                ALU.subtract, ALU.mult).then_inc(xn_done[ln], 1)

            def mid_parts(p, a):
                if p.has(2):
                    for m in range(2):
                        dve.wait_ge(res_done, count(4 * p.image(2) + a + m + 1))
                        nc.vector.tensor_copy(parts[:, 1, a + m, :], qkr[:, a + m, :]).then_inc(mid_done, 1)

            def gates(p):
                if p.has(-1):
                    i = p.image(-1)
                    for t in range(3):
                        bank = md_unit()
                        nc.vector.tensor_copy(ga[0:QT[t], t, :], bank[0:QT[t], 0:GC]).then_inc(md_free, 1)
                    if due(i):
                        dve.wait_ge(cw_done, count(i))
                    for t in range(3):
                        dve.wait_ge(md_free, count(md.so_far(t - 2)))
                        dve.sem_inc(passed, 1)
                        nc.vector.max(top[0:QT[t], t, :], ga[0:QT[t], t, 0:EXPERTS]).then_inc(top_done, 1)
                    dve.wait_ge(top_done, count(7 * i + 3))
                    nc.vector.tensor_tensor(gev[:, 0, :], top[:, :, 1], top[:, :, 0], ALU.subtract).then_inc(top_done, 1)
                    for t in range(3):
                        nc.vector.max_index(topi[0:QT[t], t, :], top[0:QT[t], t, :], ga[0:QT[t], t, 0:EXPERTS]) \
                          .then_inc(top_done, 1)

            def gate_mask(p):
                if p.has(-1):
                    i = p.image(-1)
                    dve.wait_ge(top_done, count(7 * i + 7))
                    for j in range(2):
                        nc.vector.tensor_tensor(cws[:, j, :, :], iota_e[:],
                                                topi[:, :, j:j + 1].broadcast_to([QT[0], 3, EXPERTS]),
                                                ALU.is_equal).then_inc(mask_done, 1)

            def gate_weights(p):
                if p.has(-1):
                    i = p.image(-1)
                    dve.wait_ge(gexp_done, count(i + 1))
                    nc.vector.tensor_scalar(gev[:, 2, :], gev[:, 1, :], 1.0, None, ALU.add).then_inc(gden_done, 1)
                    dve.wait_ge(gden_done, count(2 * i + 1))
                    nc.vector.reciprocal(gev[:, 3, :], gev[:, 2, :]).then_inc(gden_done, 1)

            def expert_weigh(p):
                if p.has(-1):
                    i = p.image(-1)
                    dve.wait_ge(cw_done, count(i + 1))
                    nc.vector.tensor_tensor(hw[:].rearrange("p t (e r) -> p t e r", e=EXPERTS),
                                            ga[:, :, EXPERTS:GC].rearrange("p t (e r) -> p t e r", e=EXPERTS),
                                            cws[:, 4, :, :].unsqueeze(3).broadcast_to([QT[0], 3, EXPERTS, RANK]),
                                            ALU.mult).then_inc(hw_done, 1)

            def final(p):
                if p.has(-1):
                    i = p.image(-1)
                    if due(48 * i):
                        dve.wait_ge(store, count(48 * i))
                    for t in range(3):
                        bank = md_unit()
                        nc.vector.tensor_tensor(ost[0:QT[t], t, :], bank[0:QT[t], 0:D],
                                                hres[0:QT[t], p.mod(-1, 4), t, :], ALU.add).then_inc(md_free, 1)

            def slot(p):
                for h in range(STEPS):
                    reduce_max(p, h, 0)
                    reduce_max(p, h, 1)
                    if h == 1:
                        product(p)
                        max_evac(p, 0, 1)
                    if h == 2:
                        normalise(p)
                    if h == 3:
                        layer2_evac(p)
                    if h == 5:
                        residual(p)
                    if h == 6:
                        apply(p, 2, 0, xn1)
                    if h == 7:
                        apply(p, -1, 1, xn2)
                    if h == 9:
                        max_evac(p, 1, 0)
                        gates(p)
                    if h == 10:
                        gate_mask(p)
                        mid_parts(p, 0)
                    if h == 11:
                        mid_parts(p, 2)
                    if h == 12:
                        gate_weights(p)
                    if h == 13:
                        expert_weigh(p)
                    if h == 15:
                        final(p)
                    reduce_max(p, h, 2)

            drive(dve, slot, lambda p: None, [md])

        @block.gpsimd
        def _(pool):
            nc.gpsimd.iota(iota_i[:], pattern=[[0, 3], [1, EXPERTS]], base=0, channel_multiplier=0).then_inc(setup_g, 1)
            pool.wait_ge(setup_v, SETUP_V)
            pool.wait_ge(cleared, CLEARS)

            def gather(p):
                if p.tok:
                    col, cols = CHUNKS[p.s]
                    u = 4 * p.group() + p.s
                    pool.wait_ge(raw_in, count((p.group() + 1) * RAW))
                    if due(u):
                        pool.wait_ge(rawp_read, count(u))
                    pool.sem_inc(passed, 1)
                    nc.gpsimd.tensor_scalar(rawp[:, 0:cols, :, :],
                                            raw[:, :, col:col + cols, :].rearrange("p r w q -> p w r q"), 1.0, 1.0,
                                            ALU.mult, ALU.mult).then_inc(rawp_done, 1)

            def rsqrt(p, k, ln):
                if p.has(k):
                    i = p.image(k)
                    v, y, a, b = (nw[ln][:, c, :] for c in range(4))
                    pool.wait_ge(stat[ln], count(6 * i + 6))
                    if due(3 * i):
                        pool.wait_ge(xn_done[ln], count(3 * i))
                    pool.sem_inc(passed, 1)
                    n = 0

                    def chain(ins):
                        nonlocal n
                        n += 1
                        ins.then_inc(newton[ln], 1)
                        pool.wait_ge(newton[ln], count(13 * i + n))
                        pool.sem_inc(passed, 1)

                    chain(nc.gpsimd.tensor_scalar(v, mv[ln][:, :, 1], EPS, 1.0, ALU.add, ALU.mult))
                    chain(nc.gpsimd.tensor_scalar(y.bitcast(I32), v.bitcast(I32), -0.5, RSQRT_GUESS, ALU.mult, ALU.add))
                    for step in range(3):
                        chain(nc.gpsimd.tensor_tensor(a, y, y, ALU.mult))
                        chain(nc.gpsimd.tensor_tensor(b, a, v, ALU.mult))
                        chain(nc.gpsimd.tensor_scalar(a, b, -0.5, 1.5, ALU.mult, ALU.add))
                        ins = nc.gpsimd.tensor_tensor(y, y, a, ALU.mult)
                        if step < 2:
                            chain(ins)
                    ins.then_inc(rstd[ln], 1)

            def add_constant(p):
                if p.has(2):
                    i = p.image(2)
                    pool.wait_ge(xn_done[0], count(3 * i + 3))
                    r = hres[:, p.mod(2, 4), :, :]
                    nc.gpsimd.tensor_tensor(r, r, cor[:].unsqueeze(1).broadcast_to([QT[0], 3, D]), ALU.add) \
                      .then_inc(const_added, 1)

            def max_parts(p, k, half):
                if p.has(k):
                    u = 2 * p.image(k) + half
                    pool.wait_ge(mhi_done, count(u + 1))
                    nc.gpsimd.tensor_tensor(msr[:], msf[:], msp[:, 0, :], ALU.subtract).then_inc(mchain, 1)
                    pool.wait_ge(mchain, count(2 * u + 1))
                    pool.sem_inc(passed, 1)
                    nc.gpsimd.tensor_scalar(msp[:, 1, :], msr[:], 1.0, 1.0, ALU.mult, ALU.mult).then_inc(mchain, 1)
                    pool.wait_ge(mchain, count(2 * u + 2))
                    nc.gpsimd.tensor_tensor(msp[:, 2, :], msr[:], msp[:, 1, :], ALU.subtract).then_inc(msplit, 1)

            def rests(p, a):
                if p.has(2):
                    for m in range(2):
                        pool.wait_ge(hi_done, count(4 * p.image(2) + a + m + 1))
                        nc.gpsimd.tensor_tensor(qkr[:, a + m, :], qkf[:, a + m, :], parts[:, 0, a + m, :],
                                                ALU.subtract).then_inc(res_done, 1)

            def low_parts(p, a):
                if p.has(2):
                    for m in range(2):
                        pool.wait_ge(mid_done, count(4 * p.image(2) + a + m + 1))
                        nc.gpsimd.tensor_tensor(parts[:, 2, a + m, :], qkr[:, a + m, :], parts[:, 1, a + m, :],
                                                ALU.subtract).then_inc(lo_done, 1)

            def combine(p):
                if p.has(-1):
                    i = p.image(-1)
                    pool.wait_ge(gden_done, count(2 * i + 2))
                    pool.wait_ge(mask_done, count(2 * i + 2))
                    nc.gpsimd.tensor_tensor(gev[:, 2, :], gev[:, 1, :], gev[:, 3, :], ALU.mult).then_inc(gchain, 1)
                    pool.wait_ge(gchain, count(3 * i + 1))
                    for j, w in ((0, 3), (1, 2)):
                        nc.gpsimd.tensor_tensor(cws[:, 2 + j, :, :], cws[:, j, :, :],
                                                gev[:, w, :].unsqueeze(2).broadcast_to([QT[0], 3, EXPERTS]),
                                                ALU.mult).then_inc(gchain, 1)
                    pool.wait_ge(gchain, count(3 * i + 3))
                    nc.gpsimd.tensor_tensor(cws[:, 4, :, :], cws[:, 2, :, :], cws[:, 3, :, :], ALU.add) \
                      .then_inc(cw_done, 1)

            def slot(p):
                gather(p)
                max_parts(p, 0, 1)
                rsqrt(p, 2, 0)
                rsqrt(p, -1, 1)
                add_constant(p)
                rests(p, 0)
                max_parts(p, 1, 0)
                rests(p, 2)
                low_parts(p, 0)
                low_parts(p, 2)
                combine(p)

            drive(pool, slot, gather, [])


_INS = ["x", "txt", "eye"] + ["L0_tok_" + n for n in ("W1", "b1", "W2", "b2")] \
    + ["L0_attn_" + n for n in ("Wq", "bq", "Wl", "bl", "Wk", "bk", "Wv", "bv", "Wo", "bo")] \
    + ["L0_ffn_" + n for n in ("Wg", "A", "B")]


def kernel(**inputs):
    import numpy as np
    import concourse.bacc as bacc
    from concourse.bass_utils import run_bass_kernel_spmd

    nc = bacc.Bacc("TRN2", target_bir_lowering=False, num_devices=1)
    arrays, args = {}, []
    inputs["eye"] = np.eye(128, dtype=np.float32)
    for name in _INS:
        a = np.ascontiguousarray(inputs[name])
        arrays[f"in_{name}"] = a
        args.append(nc.dram_tensor(f"in_{name}", a.shape, mybir.dt.from_np(a.dtype), kind="ExternalInput").ap())
    args.append(nc.dram_tensor("out_tokens", (IMAGES, TOK, D), F32, kind="ExternalOutput").ap())
    early_fusion(nc, *args)
    r = run_bass_kernel_spmd(nc, [arrays], core_ids=[0])
    return r.results[0]["out_tokens"]
```

```python
from contextlib import ExitStack

import concourse.bass as bass
from concourse import mybir

F32 = mybir.dt.float32
BF16 = mybir.dt.bfloat16
I32 = mybir.dt.int32
U32 = mybir.dt.uint32
ALU = mybir.AluOpType
ACT = mybir.ActivationFunctionType
AX_X = mybir.AxisListType.X

IMAGES, CH, SIDE, PATCH = 128, 3, 224, 16
GRID = SIDE // PATCH
PATCHES = GRID * GRID
TXT = 77
TOK = PATCHES + TXT
D = 256
HEADS, HD = 16, 16
LAT = D // 4
EXPERTS, RANK = 8, 16
ER = EXPERTS * RANK
EPS = 1e-5
GROUP = 4
GROUPS = IMAGES // GROUP
ROWS = GROUP * GRID
KT1 = CH * PATCH * PATCH // 128
HALF = GRID // 2
CHUNKS = [(0, 2), (2, 2), (4, 2), (6, 1)]
QT = [98, 98, TXT]
QO = [0, 98, 196]
KEYS = TOK // 3
SLOTS = 6
QPART = [0, 0, 0, 1, 1, 2]
KPART = [0, 1, 2, 0, 1, 0]
SROWS = SLOTS * HD
XROWS = SROWS + 3
VW = 32
CLEARS, SETUP_V = 10, 18
GC = EXPERTS + ER
POSITIONS = 3 * HEADS
PLAN = dict(
    max_t1=(1,), weigh3=(1, 2, 3), values=(4, 6, 10), expert_t=(5,), expert_out=(7, 8, 9),
    layer2=(11, 13), tok_t=(12, 18, 33), weigh0=(17, 19, 20), out_t=(14, 16, 18), otok_t=(21, 24),
    xn1_t=(22, 23), q=(25, 27), weigh1=(24, 26, 28), out_project=(26, 28, 30), k=(29, 31), max_t0=(32,),
    z0=(34, 35, 36), xn2_t=(38, 39), weigh2=(37, 40, 41), expert_in=(41, 43, 44), z1=(42, 43, 45),
    tanh=(0,), gate_exp=(47,), q_high=(26, 28), k_high=(30, 32),
    gate_weights=(0,), product=(1,), max_high1=(2,), expert_weigh=(3,), stats1=(12, 14, 15), aggregate1=(15,),
    apply1=(18, 19, 20), stats2=(27, 29, 31), aggregate2=(31,), q_mid=(29, 31), k_mid=(33, 35), max_high0=(33,),
    apply2=(34, 35, 36), gate_top=(42, 44, 45), gate_choice=(45,), gate_mask=(46,))
MA_SLOT, MD_SLOT = 19, 16


def early_fusion(nc, x, txt, eye, W1, b1, W2, b2, Wq, bq, Wl, bl, Wk, bk, Wv, bv, Wo, bo, Wg, A, B, out):
    ctx = ExitStack()

    def sb(name, shape, dt=F32):
        return ctx.enter_context(nc.sbuf_tensor(name, shape, dt))

    def sem(name):
        return ctx.enter_context(nc.semaphore(name))

    with ctx:
        w1 = sb("w1", [128, KT1, D])
        w2 = sb("w2", [128, 2, D])
        wq = sb("wq", [128, 2, D])
        wqp = sb("wqp", [128, 2, 2, HD, 8])
        wo = sb("wo", [128, 2, D])
        wlk = sb("wlk", [128, 2, 2, HD, 8])
        wlv = sb("wlv", [128, 2, D])
        wga = sb("wga", [128, 2, GC])
        wb = sb("wb", [ER, D])
        wl = sb("wl", [128, 2, LAT])
        wlT = sb("wlT", [LAT, 2, 128])
        wk = sb("wk", [LAT, D])
        wkv = sb("wkv", [LAT, 2, D])
        blc = sb("blc", [LAT, 1])
        b1c = sb("b1c", [128, 2])
        bqc = sb("bqc", [128, 2])
        bkc = sb("bkc", [128, 2])
        bvc = sb("bvc", [128, 2])
        bvw = sb("bvw", [128, 2, QT[0]])
        b2r = sb("b2r", [QT[0], D])
        cor = sb("cor", [QT[0], D])
        ident = sb("ident", [128, 128])
        iota_i = sb("iota_i", [QT[0], 3, EXPERTS], I32)
        iota_e = sb("iota_e", [QT[0], 3, EXPERTS])

        raw = sb("raw", [128, CH * PATCH, HALF, PATCH])
        rawp = sb("rawp", [128, 2, CH * PATCH, PATCH])
        xT = sb("xT", [128, KT1, 2, 2, ROWS])
        zring = sb("zring", [128, 2, 2, GRID, GROUP, GRID])
        tnh = sb("tnh", [128, 2, PATCHES])
        h1 = sb("h1", [128, 2, PATCHES])
        hres = sb("hres", [QT[0], 4, 3, D])
        xn1 = sb("xn1", [QT[0], 3, D])
        xn2 = sb("xn2", [QT[0], 3, D])
        xnT1 = sb("xnT1", [128, 2, TOK])
        xnT2 = sb("xnT2", [128, 2, TOK])
        qkf = sb("qkf", [128, 4, TOK])
        qkr = sb("qkr", [128, 4, TOK])
        parts = sb("parts", [128, 3, 4, TOK], BF16)
        qst = sb("qst", [XROWS, 2, HEADS, TOK], BF16)
        kst = sb("kst", [XROWS, 2, HEADS, TOK], BF16)
        mxs = sb("mxs", [KEYS, 2, 3, HEADS])
        msf = sb("msf", [8, TOK])
        msr = sb("msr", [8, TOK])
        msp = sb("msp", [8, 3, TOK], BF16)
        vaug = sb("vaug", [KEYS, 2, 3, HEADS, VW])
        prob = sb("prob", [KEYS, 2, 4, 3, TOK])
        oT = sb("oT", [128, 4, TOK])
        orec = sb("orec", [QT[0], 3, HEADS])
        otok = sb("otok", [QT[0], 3, D])
        otT = sb("otT", [128, 2, TOK])
        st = [sb(f"st{i}", [QT[0], 3, 6]) for i in range(2)]
        mv = [sb(f"mv{i}", [QT[0], 3, 2]) for i in range(2)]
        inv = [sb(f"inv{i}", [QT[0], 2, 3]) for i in range(2)]
        minus_half = sb("minus_half", [QT[0], 3])
        ga = sb("ga", [QT[0], 3, GC])
        gev = sb("gev", [QT[0], 4, 3])
        top = sb("top", [QT[0], 3, 8])
        topi = sb("topi", [QT[0], 3, 8], U32)
        cws = sb("cws", [QT[0], 5, 3, EXPERTS])
        hw = sb("hw", [QT[0], 3, ER])
        hwT = sb("hwT", [ER, TOK])
        ost = sb("ost", [QT[0], 3, D])

        ps_sm = [ctx.enter_context(nc.psum_tensor(f"ps_sm{i}", [128, 512], F32)) for i in range(2)]
        ps_st = [ctx.enter_context(nc.psum_tensor(f"ps_st{i}", [128, 512], F32)) for i in range(2)]
        ps_po = ctx.enter_context(nc.psum_tensor("ps_po", [128, 512], F32))
        ps_ma = [ctx.enter_context(nc.psum_tensor(f"ps_ma{i}", [128, 512], F32)) for i in range(2)]
        ps_md = [ctx.enter_context(nc.psum_tensor("ps_md", [128, 512], F32))]

        sm_full, sm_free = sem("sm_full"), sem("sm_free")
        st_full, exp_done = sem("st_full"), sem("exp_done")
        po_full, po_free = sem("po_full"), sem("po_free")
        ma_full, ma_free = sem("ma_full"), sem("ma_free")
        md_full, md_free = sem("md_full"), sem("md_free")
        w_in, b_in = sem("w_in"), sem("b_in")
        raw_in = sem("raw_in")
        rawp_done = sem("rawp_done")
        rawp_read = sem("rawp_read")
        raw_clear = sem("raw_clear")
        txt_in = sem("txt_in")
        stack_in = [sem(f"stack_in{i}") for i in range(4)]
        mrow_in = [sem(f"mrow_in{i}") for i in range(4)]
        store = sem("store")
        tanh_done, h1_done = sem("tanh_done"), sem("h1_done")
        stat = [sem("stat1"), sem("stat2")]
        eps_added = [sem("eps_added1"), sem("eps_added2")]
        rstd = [sem("rstd1"), sem("rstd2")]
        xn_done = [sem("xn1_done"), sem("xn2_done")]
        const_added = sem("const_added")
        hi_done, mid_done = sem("hi_done"), sem("mid_done")
        res_done, lo_done = sem("res_done"), sem("lo_done")
        mhi_done, mchain, msplit = sem("mhi_done"), sem("mchain"), sem("msplit")
        orec_done = sem("orec_done")
        top_done = sem("top_done")
        gexp_done = sem("gexp_done")
        gden_done = sem("gden_done")
        mask_done = sem("mask_done")
        gchain, cw_done = sem("gchain"), sem("cw_done")
        hw_done = sem("hw_done")
        passed = sem("passed")
        cleared, setup_pe, setup_v, setup_g = sem("cleared"), sem("setup_pe"), sem("setup_v"), sem("setup_g")

        class Linear:

            def __init__(self, turn, a, b):
                self.turn, self.a, self.b = turn, a, b

            def __add__(self, n):
                return Linear(self.turn, self.a, self.b + n)

            def __sub__(self, n):
                return Linear(self.turn, self.a, self.b - n)

            def __mul__(self, n):
                return Linear(self.turn, self.a * n, self.b * n)

            __radd__, __rmul__ = __add__, __mul__

            def value(self):
                return self.turn * self.a + self.b

        def index(v):
            return v.value() if isinstance(v, Linear) else v

        def count(v):
            assert (v.b if isinstance(v, Linear) else v) > 0
            return index(v)

        def due(v):
            return isinstance(v, Linear) or v > 0


        class Units:

            def __init__(self, banks, per_slot):
                self.banks, self.per_turn, self.count, self.g, self.start = banks, GROUP * per_slot, 0, None, 0

            def enter(self, g):
                assert self.per_turn % self.banks == 0
                self.g, self.start = g, self.count

            def leave(self, turns):
                assert self.count - self.start == self.per_turn, (self.count - self.start, self.per_turn)
                self.count, self.g = self.start + turns * self.per_turn, None

            def so_far(self, ahead=0):
                n = self.count + ahead
                return n if self.g is None else Linear(self.g, self.per_turn, n)

            def next(self):
                self.count += 1
                return (self.count - 1) % self.banks, self.so_far()

        class Slot:

            def __init__(self, g, s, tok=True):
                self.g, self.s, self.tok = g, s, tok

            def image(self, k):
                return self.g * GROUP + (2 + self.s + k)

            def place(self, k):
                return index(self.image(k))

            def mod(self, k, m):
                return (2 + self.s + k) % m

            def has(self, k):
                i = self.image(k)
                return not isinstance(i, int) or 0 <= i < IMAGES

            def group(self):
                return self.g + 2

            def landed(self, k, each):
                return (self.g * 2 + ((2 + self.s + k) // 2 + 1)) * each

        def units(kind, q):
            return [u for u, at in enumerate(PLAN[kind]) if at == q]

        TURNS = GROUPS - 2
        HEAD = [Slot(-2, s) for s in range(4)]
        FILL = [Slot(-1, s) for s in range(4)]
        DRAIN = [Slot(TURNS, s, tok=False) for s in range(4)] + [Slot(TURNS + 1, s, tok=False) for s in range(4)]

        def drive(eng, slot, tok_only, counters):
            for p in HEAD:
                tok_only(p)
            for p in FILL:
                slot(p)
            with eng.Fori(0, TURNS) as g:
                for c in counters:
                    c.enter(g)
                for s in range(4):
                    copy = eng.alloc_register(f"turn{s}")
                    eng.reg_mov(copy, g)
                    turn = eng.snap(copy, min_val=0, max_val=TURNS - 1)
                    for c in counters:
                        c.g = turn
                    slot(Slot(Linear(turn, 1, 0), s))
            for c in counters:
                c.leave(TURNS)
            for p in DRAIN:
                slot(p)

        STACK, MROW, RAW, STORE = 12 * 16, 3 * 16, 24 * 16, 3 * 16
        block = ctx.enter_context(nc.Block())

        x_v = x.rearrange("b c (gh ph) w -> b gh c ph w", ph=PATCH)
        out_v = out[:, 0:PATCHES, :].rearrange("b (gh gw) d -> b gw gh d", gw=GRID)

        @block.sync
        def _(sp):
            md = Units(1, MD_SLOT)

            def load_raw(group):
                first = group * GROUP if isinstance(group, int) else index(group) % GROUPS * GROUP
                for half in range(2):
                    for b in range(GROUP):
                        for c in range(CH):
                            row = 64 * half + b * GRID
                            sp.dma_start(raw[row:row + GRID, c * PATCH:(c + 1) * PATCH, :, :]
                                         .rearrange("p r w q -> p r (w q)"),
                                         x_v[first + b, :, c, :,
                                             half * HALF * PATCH:(half + 1) * HALF * PATCH]).then_inc(raw_in, 16)

            sp.sem_inc(store, 16)
            sp.wait_ge(raw_clear, 1)
            load_raw(0)
            sp.dma_start(ident[:], eye).then_inc(w_in, 16)
            for dst, src in ((w1, W1), (w2, W2), (wq, Wq), (wo, Wo), (wl, Wl)):
                sp.dma_start(dst[:], src.rearrange("(k p) n -> p k n", p=128)).then_inc(w_in, 16)
            sp.dma_start(wk[:], Wk).then_inc(w_in, 16)
            sp.dma_start(wkv[:, 1, :], Wv).then_inc(w_in, 16)
            sp.dma_start(wga[:, :, 0:EXPERTS], Wg.rearrange("(k p) e -> p k e", p=128)).then_inc(w_in, 16)
            for k in range(2):
                sp.dma_start(wga[:, k, EXPERTS:GC].rearrange("p (e r) -> p e r", e=EXPERTS),
                             A[:, k * 128:(k + 1) * 128, :].rearrange("e p r -> p e r")).then_inc(w_in, 16)
            sp.dma_start(wb[:], B.rearrange("e r d -> (e r) d")).then_inc(w_in, 16)
            sp.dma_start(blc[:], bl.rearrange("(p a) -> p a", a=1)).then_inc(b_in, 16)
            for dst, src in ((b1c, b1), (bvc, bv)):
                for k in range(2):
                    sp.dma_start(dst[:, k:k + 1], src[k * 128:(k + 1) * 128].rearrange("(p a) -> p a", a=1)) \
                      .then_inc(b_in, 16)
            for dst, src in ((bqc, bq), (bkc, bk)):
                for k in range(2):
                    sp.dma_start(dst[:, k:k + 1], src[k * 128:(k + 1) * 128].rearrange("(h d) -> d h", h=8),
                                 allow_slow_non_contiguous=True) \
                      .then_inc(b_in, 16)
            sp.dma_start(b2r[:], b2.rearrange("(a d) -> a d", a=1).broadcast_to([QT[0], D])).then_inc(b_in, 16)
            sp.dma_start(cor[:], bo.rearrange("(a d) -> a d", a=1).broadcast_to([QT[0], D])).then_inc(b_in, 16)
            sp.wait_ge(cleared, CLEARS)

            def reload(p):
                if p.tok and p.s == 3:
                    sp.wait_ge(rawp_done, count(4 * p.group() + 4))
                    sp.sem_inc(passed, 1)
                    load_raw(p.group() + 1)

            def text(p):
                if p.has(2):
                    if p.has(-2):
                        sp.wait_ge(md_free, count(md.so_far()))
                    sp.sem_inc(passed, 1)
                    sp.dma_start(hres[0:TXT, p.mod(2, 4), 2, :], txt[p.place(2), :, :]).then_inc(txt_in, 16)

            def max_rows(p, k, half):
                if p.has(k):
                    sp.wait_ge(msplit, count(2 * p.image(k) + half + 1))
                    sp.sem_inc(passed, 1)
                    if due(48 * p.image(k - 2) + 24 * half + 24):
                        sp.wait_ge(st_full, count(48 * p.image(k - 2) + 24 * half + 24))
                    sp.sem_inc(passed, 1)
                    y = p.mod(k, 2)
                    for r in range(3):
                        sp.dma_start(qst[SROWS + r:SROWS + r + 1, y, 8 * half:8 * half + 8, :], msp[:, r, :]) \
                          .then_inc(mrow_in[2 * y + half], 16)

            def stack(p, half):
                if p.has(2):
                    if due(48 * p.image(0) + 24 * half + 24):
                        sp.wait_ge(st_full, count(48 * p.image(0) + 24 * half + 24))
                    sp.sem_inc(passed, 1)
                    y = p.mod(2, 2)
                    for dst, t, which in ((qst, 0, QPART), (kst, 2, KPART)):
                        sp.wait_ge(hi_done, count(4 * p.image(2) + t + half + 1))
                        sp.wait_ge(mid_done, count(4 * p.image(2) + t + half + 1))
                        sp.wait_ge(lo_done, count(4 * p.image(2) + t + half + 1))
                        sp.sem_inc(passed, 1)
                        for row, part in enumerate(which):
                            sp.dma_start(dst[row * HD:(row + 1) * HD, y, 8 * half:8 * half + 8, :],
                                         parts[:, part, t + half, :]).then_inc(stack_in[2 * y + half], 16)

            def save(p):
                if p.has(-2):
                    i = p.place(-2)
                    sp.wait_ge(md_free, count(md.so_far()))
                    sp.sem_inc(passed, 1)
                    for t in range(2):
                        sp.dma_start(out_v[i, t * HALF:(t + 1) * HALF, :, :], ost[0:QT[t], t, :]).then_inc(store, 16)
                    sp.dma_start(out[i, PATCHES:TOK, :], ost[0:TXT, 2, :]).then_inc(store, 16)

            def slot(p):
                md.count += 1 * p.has(0) + 3 * p.has(-2)
                text(p)
                save(p)
                max_rows(p, 0, 1)
                reload(p)
                stack(p, 0)
                max_rows(p, 1, 0)
                stack(p, 1)
                md.count += 9 * p.has(-1) + 2 * p.has(2) + 1 * p.has(1)

            drive(sp, slot, reload, [md])
            sp.wait_ge(raw_in, (GROUPS + 1) * RAW)
            sp.wait_ge(store, STORE * IMAGES + 16)

        @block.tensor
        def _(pe):
            ma, md = Units(2, MA_SLOT), Units(1, MD_SLOT)
            ready = {}

            pe.wait_ge(w_in, 16 * 12)
            pe.wait_ge(b_in, 16 * 11)
            for k in range(2):
                last = nc.tensor.transpose(ps_md[0][0:LAT, k * 128:(k + 1) * 128], wl[:, k, :], ident[:])
            last.then_inc(setup_pe, 1)
            pe.wait_ge(setup_v, 3)
            for k in range(2):
                nc.tensor.matmul(ps_sm[k][:, :], wlT[:, k, :], wkv[:, :, :].rearrange("p a n -> p (a n)"),
                                 start=True, stop=True)
            for a in range(2):
                for k in range(2):
                    last = nc.tensor.matmul(ps_st[a][:, k:k + 1], wkv[:, a, k * 128:(k + 1) * 128], blc[:],
                                            start=(k == 0), stop=True, skip_group_check=True)
            last.then_inc(setup_pe, 1)
            pe.wait_ge(setup_v, 14)
            for k in range(2):
                last = nc.tensor.matmul(ps_md[0][0:QT[0], 0:D], bvw[:, k, :], wo[:, k, :],
                                        start=(k == 0), stop=(k == 1))
            last.then_inc(setup_pe, 1)
            pe.wait_ge(setup_v, SETUP_V)
            pe.wait_ge(cleared, CLEARS)

            def ma_unit():
                bank, n = ma.next()
                if due(ma.so_far(-2)):
                    pe.wait_ge(ma_free, count(ma.so_far(-2)))
                return ps_ma[bank]

            def md_unit():
                bank, n = md.next()
                if due(md.so_far(-1)):
                    pe.wait_ge(md_free, count(md.so_far(-1)))
                return ps_md[bank]

            def tok_transpose(p, u):
                if p.tok:
                    cols = CHUNKS[p.s][1]
                    pe.wait_ge(rawp_done, count(4 * p.group() + p.s + 1))
                    bank = ma_unit()
                    pe.sem_inc(passed, 1)
                    for j in range(2):
                        k = 2 * u + j
                        for w in range(cols):
                            a = (j * cols + w) * 128
                            last = nc.tensor.transpose(bank[:, a:a + 128],
                                                       rawp[:, w, 8 * k:8 * k + 8, :]
                                                       .rearrange("p r q -> p (r q)"), ident[:])
                    last.then_inc(ma_full, 1)
                    ready["xT"] = ma.so_far()

            def tok_layer1(p, m, u):
                if p.tok:
                    n = 2 * CHUNKS[p.s][1] * ROWS
                    if u == 0:
                        pe.wait_ge(ma_free, count(ready["xT"]))
                        ready["z"] = ma_unit()
                    for k in (2 * u, 2 * u + 1):
                        last = nc.tensor.matmul(ready["z"][:, 0:n], w1[:, k, m * 128:(m + 1) * 128],
                                                xT[:, k, 0:n // (2 * ROWS), :, :].rearrange("p w a n -> p (w a n)"),
                                                start=(k == 0), stop=(k == KT1 - 1))
                        if m == 0 and k == 0:
                            last.then_inc(rawp_read, 1)
                    if u == KT1 // 2 - 1:
                        last.then_inc(ma_full, 1)

            def layer2(p, t):
                if p.has(2):
                    pe.wait_ge(h1_done, count(p.image(2) + 1))
                    bank = md_unit()
                    for k in range(2):
                        last = nc.tensor.matmul(bank[0:QT[t], 0:D], h1[:, k, QO[t]:QO[t] + QT[t]], w2[:, k, :],
                                                start=(k == 0), stop=(k == 1))
                    last.then_inc(md_full, 1)

            def feature_major(src, f):
                bank = ma_unit()
                for t in range(3):
                    last = nc.tensor.transpose(bank[:, QO[t]:QO[t] + QT[t]],
                                               src[0:QT[t], t, f * 128:(f + 1) * 128], ident[0:QT[t], 0:QT[t]])
                last.then_inc(ma_full, 1)

            def xn_transpose(p, k, ln, src, f):
                if p.has(k):
                    pe.wait_ge(xn_done[ln], count(3 * p.image(k) + 3))
                    feature_major(src, f)
                    ready[f"xnT{ln}"] = ma.so_far()

            def project(p, w, m):
                if p.has(2):
                    pe.wait_ge(ma_free, count(ready["xnT0"]))
                    bank = ma_unit()
                    for k in range(2):
                        last = nc.tensor.matmul(bank[:, 0:TOK], w[:, k, m, :, :].rearrange("p d h -> p (d h)"),
                                                xnT1[:, k, :], start=(k == 0), stop=(k == 1))
                    last.then_inc(ma_full, 1)

            def values(p, t):
                if p.has(1):
                    bank = ma_unit()
                    for k in range(2):
                        last = nc.tensor.matmul(bank[0:KEYS, 0:D], xnT1[:, k, t * KEYS:(t + 1) * KEYS],
                                                wlv[:, k, :], start=(k == 0), stop=(k == 1))
                    last.then_inc(ma_full, 1)

            def max_scores(p, h, t):
                if p.has(1):
                    y = p.mod(1, 2)
                    if h % 8 == 0 and t == 0:
                        pe.wait_ge(stack_in[2 * y + h // 8], count(p.landed(1, STACK)))
                    bank = (3 * h + t) % 2
                    if due(48 * p.image(1) + 3 * h + t - 1):
                        pe.wait_ge(sm_free, count(48 * p.image(1) + 3 * h + t - 1))
                    nc.tensor.matmul(ps_sm[bank][0:KEYS, 0:TOK], qst[0:SROWS, y, h, t * KEYS:(t + 1) * KEYS],
                                     kst[0:SROWS, y, h, :], start=True, stop=True).then_inc(sm_full, 1)

            def key_scores(p, h, t):
                if p.has(0):
                    y = p.mod(0, 2)
                    if h % 8 == 0 and t == 0:
                        pe.wait_ge(mrow_in[2 * y + h // 8], count(p.landed(0, MROW)))
                    bank = (3 * h + t) % 2
                    if due(48 * p.image(0) + 3 * h + t - 1):
                        pe.wait_ge(exp_done, count(48 * p.image(0) + 3 * h + t - 1))
                    nc.tensor.matmul(ps_st[bank][0:KEYS, 0:TOK], kst[:, y, h, t * KEYS:(t + 1) * KEYS],
                                     qst[:, y, h, :], start=True, stop=True).then_inc(st_full, 1)

            def max_transpose(p, k, half):
                if p.has(k):
                    pe.wait_ge(sm_free, count(48 * p.image(k) + 24 * half + 24))
                    bank = md_unit()
                    for t in range(3):
                        last = nc.tensor.transpose(bank[0:8, t * KEYS:(t + 1) * KEYS],
                                                   mxs[:, p.mod(k, 2), t, 8 * half:8 * half + 8],
                                                   ident[0:KEYS, 0:KEYS])
                    last.then_inc(md_full, 1)

            def weigh(p, k, g, t):
                if p.has(k):
                    i, y = p.image(k), p.mod(k, 2)
                    if t == 0:
                        pe.wait_ge(exp_done, count(48 * i + 12 * g + 12))
                        if due(4 * i + g):
                            pe.wait_ge(po_free, count(4 * i + g))
                    for j in range(4):
                        last = nc.tensor.matmul(ps_po[VW * j:VW * (j + 1), 0:TOK], vaug[:, y, t, 4 * g + j, :],
                                                prob[:, g % 2, j, t, :], start=(t == 0), stop=(t == 2))
                    if t == 2:
                        last.then_inc(po_full, 1)

            def out_transpose(p, t):
                if p.has(-1):
                    pe.wait_ge(po_free, count(4 * p.image(-1) + 4))
                    bank = md_unit()
                    for g in range(4):
                        last = nc.tensor.transpose(bank[0:QT[t], g * 128:(g + 1) * 128],
                                                   oT[:, g, QO[t]:QO[t] + QT[t]], ident[:])
                    last.then_inc(md_full, 1)
                    ready["otok"] = md.so_far()

            def otok_transpose(p, f):
                if p.has(-1):
                    pe.wait_ge(md_free, count(ready["otok"]))
                    feature_major(otok, f)
                    ready["otT"] = ma.so_far()

            def out_project(p, t):
                if p.has(-1):
                    pe.wait_ge(ma_free, count(ready["otT"]))
                    bank = md_unit()
                    for k in range(2):
                        last = nc.tensor.matmul(bank[0:QT[t], 0:D], otT[:, k, QO[t]:QO[t] + QT[t]], wo[:, k, :],
                                                start=(k == 0), stop=(k == 1))
                    last.then_inc(md_full, 1)

            def expert_in(p, t):
                if p.has(-1):
                    pe.wait_ge(ma_free, count(ready["xnT1"]))
                    bank = md_unit()
                    for k in range(2):
                        last = nc.tensor.matmul(bank[0:QT[t], 0:GC], xnT2[:, k, QO[t]:QO[t] + QT[t]],
                                                wga[:, k, :], start=(k == 0), stop=(k == 1))
                    last.then_inc(md_full, 1)

            def expert_transpose(p):
                if p.has(-2):
                    pe.wait_ge(hw_done, count(p.image(-2) + 1))
                    bank = ma_unit()
                    for t in range(3):
                        last = nc.tensor.transpose(bank[:, QO[t]:QO[t] + QT[t]], hw[0:QT[t], t, :],
                                                   ident[0:QT[t], 0:QT[t]])
                    last.then_inc(ma_full, 1)
                    ready["hwT"] = ma.so_far()

            def expert_out(p, t):
                if p.has(-2):
                    pe.wait_ge(ma_free, count(ready["hwT"]))
                    bank = md_unit()
                    nc.tensor.matmul(bank[0:QT[t], 0:D], hwT[:, QO[t]:QO[t] + QT[t]], wb[:],
                                     start=True, stop=True).then_inc(md_full, 1)

            def slot(p):
                for q in range(POSITIONS):
                    max_scores(p, q // 3, q % 3)
                    key_scores(p, q // 3, q % 3)
                    for _ in units("max_t1", q):
                        max_transpose(p, 0, 1)
                    for t in units("weigh3", q):
                        weigh(p, -1, 3, t)
                    for t in units("values", q):
                        values(p, t)
                    for _ in units("expert_t", q):
                        expert_transpose(p)
                    for t in units("expert_out", q):
                        expert_out(p, t)
                    for t in units("layer2", q):
                        layer2(p, t)
                    for u in units("tok_t", q):
                        tok_transpose(p, u)
                    for t in units("weigh0", q):
                        weigh(p, 0, 0, t)
                    for t in units("out_t", q):
                        out_transpose(p, t)
                    for f in units("otok_t", q):
                        otok_transpose(p, f)
                    for f in units("xn1_t", q):
                        xn_transpose(p, 2, 0, xn1, f)
                    for m in units("q", q):
                        project(p, wqp, m)
                    for t in units("weigh1", q):
                        weigh(p, 0, 1, t)
                    for t in units("out_project", q):
                        out_project(p, t)
                    for m in units("k", q):
                        project(p, wlk, m)
                    for _ in units("max_t0", q):
                        max_transpose(p, 1, 0)
                    for u in units("z0", q):
                        tok_layer1(p, 0, u)
                    for f in units("xn2_t", q):
                        xn_transpose(p, -1, 1, xn2, f)
                    for t in units("weigh2", q):
                        weigh(p, 0, 2, t)
                    for t in units("expert_in", q):
                        expert_in(p, t)
                    for u in units("z1", q):
                        tok_layer1(p, 1, u)

            def tok_only(p):
                for u in range(KT1 // 2):
                    tok_transpose(p, u)
                for m in range(2):
                    for u in range(KT1 // 2):
                        tok_layer1(p, m, u)

            drive(pe, slot, tok_only, [ma, md])

        @block.scalar
        def _(act):
            ma = Units(2, MA_SLOT)
            ready = {}

            def ma_unit():
                bank, n = ma.next()
                act.wait_ge(ma_full, count(n))
                return ps_ma[bank]

            act.wait_ge(setup_v, SETUP_V)
            act.wait_ge(cleared, CLEARS)

            def tok_evac(p, u):
                if p.tok:
                    cols = CHUNKS[p.s][1]
                    bank = ma_unit()
                    nc.scalar.activation(xT[:, 2 * u:2 * u + 2, 0:cols, :, :].rearrange("p j w a n -> p (j w) a n"),
                                         bank[:, 0:2 * cols * 128].rearrange("p (t a n) -> p t a n", a=2, n=64)
                                         [:, :, :, 0:ROWS], ACT.Copy).then_inc(ma_free, 1)

            def z_evac(p, m):
                if p.tok:
                    col, cols = CHUNKS[p.s]
                    if m == 0 and p.s == 0:
                        if due((p.group() - 1) * GROUP):
                            act.wait_ge(h1_done, count((p.group() - 1) * GROUP))
                    bank = ma_unit()
                    nc.scalar.activation(zring[:, index(p.group()) % 2, m, :, :, :].rearrange("p (a w) b g -> p w a (b g)", a=2)
                                         [:, col:col + cols, :, :],
                                         bank[:, 0:2 * cols * ROWS].rearrange("p (w a n) -> p w a n", a=2, w=cols),
                                         ACT.Identity, bias=b1c[:, m:m + 1]).then_inc(ma_free, 1)

            def tanh(p):
                if p.has(2):
                    act.wait_ge(ma_free, count(ma.so_far()))
                    if due(p.image(1) + 1):
                        act.wait_ge(h1_done, count(p.image(1) + 1))
                    z = zring[:, index(p.group() - 1) % 2, :, :, p.s, :]
                    nc.scalar.activation(tnh[:].rearrange("p m (w g) -> p m w g", w=GRID), z, ACT.Tanh,
                                         scale=0.5).then_inc(tanh_done, 1)

            def value_evac(p, t):
                if p.has(1):
                    bank = ma_unit()
                    nc.scalar.activation(vaug[:, p.mod(1, 2), t, :, 0:HD],
                                         bank[0:KEYS, 0:D].rearrange("p (h d) -> p h d", h=HEADS),
                                         ACT.Copy).then_inc(ma_free, 1)

            def feature_evac(p, k, dst, f):
                if p.has(k):
                    bank = ma_unit()
                    nc.scalar.activation(dst[:, f, :], bank[:, 0:TOK], ACT.Copy).then_inc(ma_free, 1)

            def qk_evac(p, u, bias):
                if p.has(2):
                    i = p.image(2)
                    if u == 0 and due(4 * i):
                        act.wait_ge(res_done, count(4 * i))
                        act.wait_ge(lo_done, count(4 * i))
                    bank = ma_unit()
                    nc.scalar.activation(qkf[:, u, :], bank[:, 0:TOK], ACT.Identity,
                                         bias=bias[:, u % 2:u % 2 + 1]).then_inc(ma_free, 1)
                    ready["qk", u] = ma.so_far()

            def high_part(p, u):
                if p.has(2):
                    if u == 0 and due(p.image(2)):
                        for half in range(2):
                            act.wait_ge(stack_in[2 * p.mod(1, 2) + half], count(p.landed(1, STACK)))
                    act.wait_ge(ma_free, count(ready["qk", u]))
                    nc.scalar.activation(parts[:, 0, u, :], qkf[:, u, :], ACT.Copy).then_inc(hi_done, 1)

            def expscore(p, h, t):
                if p.has(0):
                    i, g = p.image(0), h // 4
                    if h % 4 == 0 and t == 0:
                        if due(4 * i + g - 1):
                            act.wait_ge(po_full, count(4 * i + g - 1))
                    act.wait_ge(st_full, count(48 * i + 3 * h + t + 1))
                    nc.scalar.activation(prob[:, g % 2, h % 4, t, :], ps_st[(3 * h + t) % 2][0:KEYS, 0:TOK], ACT.Exp,
                                         scale=HD ** -0.5).then_inc(exp_done, 1)

            def out_evac(p, k, g):
                if p.has(k):
                    act.wait_ge(po_full, count(4 * p.image(k) + g + 1))
                    nc.scalar.activation(oT[:, g, :], ps_po[:, 0:TOK], ACT.Copy).then_inc(po_free, 1)

            def gate_exp(p):
                if p.has(-1):
                    i = p.image(-1)
                    act.wait_ge(top_done, count(7 * i + 4))
                    if due(i):
                        act.wait_ge(cw_done, count(i))
                    nc.scalar.activation(gev[:, 1, :], gev[:, 0, :], ACT.Exp).then_inc(gexp_done, 1)

            def expert_evac(p):
                if p.has(-2):
                    bank = ma_unit()
                    nc.scalar.activation(hwT[:, :], bank[:, 0:TOK], ACT.Copy).then_inc(ma_free, 1)

            def slot(p):
                for q in range(POSITIONS):
                    expscore(p, q // 3, q % 3)
                    for _ in units("tanh", q):
                        tanh(p)
                    if q == PLAN["weigh3"][2]:
                        out_evac(p, -1, 3)
                    for t in units("values", q):
                        value_evac(p, t)
                    for _ in units("expert_t", q):
                        expert_evac(p)
                    for u in units("tok_t", q):
                        tok_evac(p, u)
                    if q == PLAN["weigh0"][2]:
                        out_evac(p, 0, 0)
                    for f in units("otok_t", q):
                        feature_evac(p, -1, otT, f)
                    for f in units("xn1_t", q):
                        feature_evac(p, 2, xnT1, f)
                    for m in units("q", q):
                        qk_evac(p, m, bqc)
                    for m in units("q_high", q):
                        high_part(p, m)
                    if q == PLAN["weigh1"][2]:
                        out_evac(p, 0, 1)
                    for m in units("k", q):
                        qk_evac(p, 2 + m, bkc)
                    for m in units("k_high", q):
                        high_part(p, 2 + m)
                    if q == PLAN["z0"][2]:
                        z_evac(p, 0)
                    for f in units("xn2_t", q):
                        feature_evac(p, -1, xnT2, f)
                    if q == PLAN["weigh2"][2]:
                        out_evac(p, 0, 2)
                    if q == PLAN["z1"][2]:
                        z_evac(p, 1)
                    for _ in units("gate_exp", q):
                        gate_exp(p)

            def tok_only(p):
                for u in range(KT1 // 2):
                    tok_evac(p, u)
                z_evac(p, 0)
                z_evac(p, 1)

            drive(act, slot, tok_only, [ma])

        @block.vector
        def _(dve):
            md = Units(1, MD_SLOT)
            ready = {}

            def md_unit():
                bank, n = md.next()
                dve.wait_ge(md_full, count(n))
                return ps_md[bank]

            nc.vector.memset(raw[:], 0.0).then_inc(raw_clear, 1)
            for c in range(2):
                nc.vector.memset(mv[c][:], 0.0).then_inc(cleared, 1)
            nc.vector.memset(hres[:], 0.0).then_inc(cleared, 1)
            nc.vector.memset(ga[:], 0.0).then_inc(cleared, 1)
            nc.vector.memset(top[:], 0.0).then_inc(cleared, 1)
            nc.vector.memset(topi[:], 0).then_inc(cleared, 1)
            nc.vector.memset(minus_half[:], -0.5).then_inc(cleared, 1)
            nc.vector.memset(vaug[:], 0.0).then_inc(cleared, 1)
            nc.vector.memset(kst[SROWS:XROWS, :, :, :], 1.0).then_inc(cleared, 1)
            dve.wait_ge(cleared, CLEARS - 1)
            nc.vector.memset(vaug[:, :, :, :, HD:HD + 1], 1.0).then_inc(cleared, 1)

            dve.wait_ge(w_in, 16 * 12)
            for m in range(2):
                nc.vector.tensor_copy(wkv[:, 0, m * 128:(m + 1) * 128].rearrange("p (d h) -> p d h", h=8),
                                      wk[:, m * 128:(m + 1) * 128].rearrange("p (h d) -> p d h", h=8)) \
                  .then_inc(setup_v, 1)
            dve.wait_ge(setup_pe, 1)
            nc.vector.tensor_copy(wlT[:], ps_md[0][0:LAT, 0:256].rearrange("p (k n) -> p k n", k=2)).then_inc(setup_v, 1)
            dve.wait_ge(setup_pe, 2)
            dve.wait_ge(b_in, 16 * 11)
            for k in range(2):
                nc.vector.tensor_copy(wlk[:, k, :, :, :].rearrange("p m d h -> p (m d h)"), ps_sm[k][:, 0:D]) \
                  .then_inc(setup_v, 1)
                for m in range(2):
                    nc.vector.tensor_copy(wqp[:, k, m, :, :], wq[:, k, m * 128:(m + 1) * 128]
                                          .rearrange("p (h d) -> p d h", h=8)).then_inc(setup_v, 1)
                nc.vector.tensor_copy(wlv[:, k, :], ps_sm[k][:, D:2 * D]).then_inc(setup_v, 1)
            nc.vector.tensor_tensor(bvc[:], bvc[:], ps_st[1][:, 0:2], ALU.add).then_inc(setup_v, 1)
            dve.wait_ge(setup_v, 12)
            for k in range(2):
                nc.vector.tensor_copy(bvw[:, k, :], bvc[:, k:k + 1].broadcast_to([128, QT[0]])).then_inc(setup_v, 1)
            nc.vector.tensor_tensor(bkc[:], bkc[:], ps_st[0][:, 0:2], ALU.add).then_inc(setup_v, 1)
            nc.vector.tensor_scalar(w2[:], w2[:], 0.5, None, ALU.mult).then_inc(setup_v, 1)
            dve.wait_ge(setup_g, 1)
            nc.vector.tensor_copy(iota_e[:], iota_i[:]).then_inc(setup_v, 1)
            dve.wait_ge(setup_pe, 3)
            nc.vector.tensor_tensor(cor[:], cor[:], ps_md[0][0:QT[0], 0:D], ALU.add).then_inc(setup_v, 1)

            def product(p):
                if p.has(2):
                    dve.wait_ge(tanh_done, count(p.image(2) + 1))
                    z = zring[:, index(p.group() - 1) % 2, :, :, p.s, :].rearrange("p m w g -> p (m w) g")
                    nc.vector.scalar_tensor_tensor(h1[:].rearrange("p m (w g) -> p (m w) g", w=GRID),
                                                   tnh[:].rearrange("p m (w g) -> p (m w) g", w=GRID), 1.0, z,
                                                   ALU.add, ALU.mult).then_inc(h1_done, 1)

            def reduce_max(p, h, t):
                if p.has(1):
                    dve.wait_ge(sm_full, count(48 * p.image(1) + 3 * h + t + 1))
                    nc.vector.tensor_reduce(mxs[:, p.mod(1, 2), t, h:h + 1], ps_sm[(3 * h + t) % 2][0:KEYS, 0:TOK],
                                            AX_X, ALU.max, negate=True).then_inc(sm_free, 1)

            def max_evac(p, k, half):
                if p.has(k):
                    if due(2 * p.image(k) + half):
                        dve.wait_ge(msplit, count(2 * p.image(k) + half))
                    bank = md_unit()
                    nc.vector.tensor_copy(msf[:], bank[0:8, 0:TOK]).then_inc(md_free, 1)
                    ready["msf"] = md.so_far()

            def max_high(p, k, half):
                if p.has(k):
                    dve.wait_ge(md_free, count(ready["msf"]))
                    if due(2 * p.image(k) + half):
                        kk, hh = (k, 0) if half else (k - 1, 1)
                        dve.wait_ge(mrow_in[2 * p.mod(kk, 2) + hh], count(p.landed(kk, MROW)))
                    nc.vector.tensor_copy(msp[:, 0, :], msf[:]).then_inc(mhi_done, 1)

            def normalise(p, t):
                if p.has(-1):
                    bank = md_unit()
                    v = bank[0:QT[t], :].rearrange("p (h w) -> p h w", h=HEADS)
                    nc.vector.reciprocal(orec[0:QT[t], t, :], v[:, :, HD:HD + 1].rearrange("p h w -> p (h w)")) \
                      .then_inc(orec_done, 1)
                    dve.wait_ge(orec_done, count(3 * p.image(-1) + t + 1))
                    nc.vector.tensor_tensor(otok[0:QT[t], t, :].rearrange("p (h d) -> p h d", h=HEADS),
                                            v[:, :, 0:HD],
                                            orec[0:QT[t], t, :].unsqueeze(2).broadcast_to([QT[t], HEADS, HD]),
                                            ALU.mult).then_inc(md_free, 1)

            def statistics(p, k, ln, t):
                if p.has(k):
                    if ln == 0 and t == 2:
                        dve.wait_ge(txt_in, count(16 * p.image(k) + 16))
                    else:
                        dve.wait_ge(md_free, count(ready["hres", t]))
                    nc.vector.bn_stats(st[ln][0:QT[t], t, :], hres[0:QT[t], p.mod(k, 4), t, :]).then_inc(stat[ln], 1)

            def aggregate(p, k, ln):
                if p.has(k):
                    for t in range(3):
                        dve.wait_ge(stat[ln], count(6 * p.image(k) + t + 1))
                        dve.sem_inc(passed, 1)
                        nc.vector.bn_aggr(mv[ln][0:QT[t], t, :], st[ln][0:QT[t], t, :]).then_inc(stat[ln], 1)

            def layer2_evac(p, t):
                if p.has(2):
                    bank = md_unit()
                    nc.vector.tensor_tensor(hres[0:QT[t], p.mod(2, 4), t, :], bank[0:QT[t], 0:D], b2r[0:QT[t], :],
                                            ALU.add).then_inc(md_free, 1)
                    ready["hres", t] = md.so_far()

            def residual(p, t):
                if p.has(-1):
                    dve.wait_ge(const_added, count(p.image(-1) + 1))
                    bank = md_unit()
                    r = hres[0:QT[t], p.mod(-1, 4), t, :]
                    nc.vector.tensor_tensor(r, bank[0:QT[t], 0:D], r, ALU.add).then_inc(md_free, 1)
                    ready["hres", t] = md.so_far()

            def apply(p, k, ln, dst, t):
                if p.has(k):
                    if t == 0:
                        dve.wait_ge(rstd[ln], count(p.image(k) + 1))
                    nc.vector.tensor_scalar(dst[0:QT[t], t, :], hres[0:QT[t], p.mod(k, 4), t, :],
                                            mv[ln][0:QT[t], t, 0:1], inv[ln][0:QT[t], 1, t:t + 1],
                                            ALU.subtract, ALU.mult).then_inc(xn_done[ln], 1)

            def mid_part(p, u):
                if p.has(2):
                    dve.wait_ge(res_done, count(4 * p.image(2) + u + 1))
                    nc.vector.tensor_copy(parts[:, 1, u, :], qkr[:, u, :]).then_inc(mid_done, 1)

            def gates(p, t):
                if p.has(-1):
                    bank = md_unit()
                    nc.vector.tensor_copy(ga[0:QT[t], t, :], bank[0:QT[t], 0:GC]).then_inc(md_free, 1)
                    ready["ga", t] = md.so_far()

            def gate_top(p, t):
                if p.has(-1):
                    if due(p.image(-1)):
                        dve.wait_ge(cw_done, count(p.image(-1)))
                    dve.wait_ge(md_free, count(ready["ga", t]))
                    dve.sem_inc(passed, 1)
                    nc.vector.max(top[0:QT[t], t, :], ga[0:QT[t], t, 0:EXPERTS]).then_inc(top_done, 1)

            def gate_choice(p):
                if p.has(-1):
                    i = p.image(-1)
                    dve.wait_ge(top_done, count(7 * i + 3))
                    nc.vector.tensor_tensor(gev[:, 0, :], top[:, :, 1], top[:, :, 0], ALU.subtract).then_inc(top_done, 1)
                    for t in range(3):
                        nc.vector.max_index(topi[0:QT[t], t, :], top[0:QT[t], t, :], ga[0:QT[t], t, 0:EXPERTS]) \
                          .then_inc(top_done, 1)

            def gate_mask(p):
                if p.has(-1):
                    i = p.image(-1)
                    dve.wait_ge(top_done, count(7 * i + 7))
                    for j in range(2):
                        nc.vector.tensor_tensor(cws[:, j, :, :], iota_e[:],
                                                topi[:, :, j:j + 1].broadcast_to([QT[0], 3, EXPERTS]),
                                                ALU.is_equal).then_inc(mask_done, 1)

            def gate_weights(p):
                if p.has(-2):
                    i = p.image(-2)
                    dve.wait_ge(gexp_done, count(i + 1))
                    nc.vector.tensor_scalar(gev[:, 2, :], gev[:, 1, :], 1.0, None, ALU.add).then_inc(gden_done, 1)
                    dve.wait_ge(gden_done, count(2 * i + 1))
                    nc.vector.reciprocal(gev[:, 3, :], gev[:, 2, :]).then_inc(gden_done, 1)

            def expert_weigh(p):
                if p.has(-2):
                    dve.wait_ge(cw_done, count(p.image(-2) + 1))
                    nc.vector.tensor_tensor(hw[:].rearrange("p t (e r) -> p t e r", e=EXPERTS),
                                            ga[:, :, EXPERTS:GC].rearrange("p t (e r) -> p t e r", e=EXPERTS),
                                            cws[:, 4, :, :].unsqueeze(3).broadcast_to([QT[0], 3, EXPERTS, RANK]),
                                            ALU.mult).then_inc(hw_done, 1)

            def final(p, t):
                if p.has(-2):
                    if t == 0:
                        dve.wait_ge(store, count(STORE * p.image(-2) + 16))
                    bank = md_unit()
                    nc.vector.tensor_tensor(ost[0:QT[t], t, :], bank[0:QT[t], 0:D],
                                            hres[0:QT[t], p.mod(-2, 4), t, :], ALU.add).then_inc(md_free, 1)

            def slot(p):
                for q in range(POSITIONS):
                    reduce_max(p, q // 3, q % 3)
                    for _ in units("gate_weights", q):
                        gate_weights(p)
                    for _ in units("product", q):
                        product(p)
                    for _ in units("max_t1", q):
                        max_evac(p, 0, 1)
                    for _ in units("max_high1", q):
                        max_high(p, 0, 1)
                    for _ in units("expert_weigh", q):
                        expert_weigh(p)
                    for t in units("expert_out", q):
                        final(p, t)
                    for t in units("layer2", q):
                        layer2_evac(p, t)
                    for t in units("stats1", q):
                        statistics(p, 2, 0, t)
                    for _ in units("aggregate1", q):
                        aggregate(p, 2, 0)
                    for t in units("out_t", q):
                        normalise(p, t)
                    for t in units("apply1", q):
                        apply(p, 2, 0, xn1, t)
                    for t in units("out_project", q):
                        residual(p, t)
                    for t in units("stats2", q):
                        statistics(p, -1, 1, t)
                    for _ in units("aggregate2", q):
                        aggregate(p, -1, 1)
                    for m in units("q_mid", q):
                        mid_part(p, m)
                    for m in units("k_mid", q):
                        mid_part(p, 2 + m)
                    for _ in units("max_t0", q):
                        max_evac(p, 1, 0)
                    for _ in units("max_high0", q):
                        max_high(p, 1, 0)
                    for t in units("apply2", q):
                        apply(p, -1, 1, xn2, t)
                    for t in units("expert_in", q):
                        gates(p, t)
                    for t in units("gate_top", q):
                        gate_top(p, t)
                    for _ in units("gate_choice", q):
                        gate_choice(p)
                    for _ in units("gate_mask", q):
                        gate_mask(p)

            drive(dve, slot, lambda p: None, [md])

        @block.gpsimd
        def _(pool):
            nc.gpsimd.iota(iota_i[:], pattern=[[0, 3], [1, EXPERTS]], base=0, channel_multiplier=0).then_inc(setup_g, 1)
            pool.wait_ge(setup_v, SETUP_V)
            pool.wait_ge(cleared, CLEARS)

            def gather(p):
                if p.tok:
                    col, cols = CHUNKS[p.s]
                    u = 4 * p.group() + p.s
                    pool.wait_ge(raw_in, count((p.group() + 1) * RAW))
                    if due(u):
                        pool.wait_ge(rawp_read, count(u))
                    pool.sem_inc(passed, 1)
                    nc.gpsimd.tensor_scalar(rawp[:, 0:cols, :, :],
                                            raw[:, :, col:col + cols, :].rearrange("p r w q -> p w r q"), 1.0, 1.0,
                                            ALU.mult, ALU.mult).then_inc(rawp_done, 1)

            def rsqrt(p, k, ln):
                if p.has(k):
                    i = p.image(k)
                    pool.wait_ge(stat[ln], count(6 * i + 6))
                    if due(3 * i):
                        pool.wait_ge(xn_done[ln], count(3 * i))
                    pool.sem_inc(passed, 1)
                    nc.gpsimd.tensor_scalar(inv[ln][:, 0, :], mv[ln][:, :, 1], EPS, 1.0, ALU.add, ALU.mult) \
                      .then_inc(eps_added[ln], 1)
                    pool.wait_ge(eps_added[ln], count(i + 1))
                    nc.gpsimd.tensor_tensor(inv[ln][:, 1, :], inv[ln][:, 0, :], minus_half[:], ALU.pow) \
                      .then_inc(rstd[ln], 1)

            def add_constant(p):
                if p.has(2):
                    i = p.image(2)
                    pool.wait_ge(xn_done[0], count(3 * i + 3))
                    r = hres[:, p.mod(2, 4), :, :]
                    nc.gpsimd.tensor_tensor(r, r, cor[:].unsqueeze(1).broadcast_to([QT[0], 3, D]), ALU.add) \
                      .then_inc(const_added, 1)

            def max_parts(p, k, half):
                if p.has(k):
                    u = 2 * p.image(k) + half
                    pool.wait_ge(mhi_done, count(u + 1))
                    nc.gpsimd.tensor_tensor(msr[:], msf[:], msp[:, 0, :], ALU.subtract).then_inc(mchain, 1)
                    pool.wait_ge(mchain, count(2 * u + 1))
                    pool.sem_inc(passed, 1)
                    nc.gpsimd.tensor_scalar(msp[:, 1, :], msr[:], 1.0, 1.0, ALU.mult, ALU.mult).then_inc(mchain, 1)
                    pool.wait_ge(mchain, count(2 * u + 2))
                    nc.gpsimd.tensor_tensor(msp[:, 2, :], msr[:], msp[:, 1, :], ALU.subtract).then_inc(msplit, 1)

            def rest(p, u):
                if p.has(2):
                    pool.wait_ge(hi_done, count(4 * p.image(2) + u + 1))
                    nc.gpsimd.tensor_tensor(qkr[:, u, :], qkf[:, u, :], parts[:, 0, u, :],
                                            ALU.subtract).then_inc(res_done, 1)

            def low_part(p, u):
                if p.has(2):
                    pool.wait_ge(mid_done, count(4 * p.image(2) + u + 1))
                    nc.gpsimd.tensor_tensor(parts[:, 2, u, :], qkr[:, u, :], parts[:, 1, u, :],
                                            ALU.subtract).then_inc(lo_done, 1)

            def combine(p):
                if p.has(-2):
                    i = p.image(-2)
                    pool.wait_ge(gden_done, count(2 * i + 2))
                    pool.wait_ge(mask_done, count(2 * i + 2))
                    nc.gpsimd.tensor_tensor(gev[:, 2, :], gev[:, 1, :], gev[:, 3, :], ALU.mult).then_inc(gchain, 1)
                    pool.wait_ge(gchain, count(3 * i + 1))
                    for j, w in ((0, 3), (1, 2)):
                        nc.gpsimd.tensor_tensor(cws[:, 2 + j, :, :], cws[:, j, :, :],
                                                gev[:, w, :].unsqueeze(2).broadcast_to([QT[0], 3, EXPERTS]),
                                                ALU.mult).then_inc(gchain, 1)
                    pool.wait_ge(gchain, count(3 * i + 3))
                    nc.gpsimd.tensor_tensor(cws[:, 4, :, :], cws[:, 2, :, :], cws[:, 3, :, :], ALU.add) \
                      .then_inc(cw_done, 1)

            def slot(p):
                combine(p)
                max_parts(p, 0, 1)
                gather(p)
                rsqrt(p, 2, 0)
                add_constant(p)
                rest(p, 0)
                rest(p, 1)
                rsqrt(p, -1, 1)
                low_part(p, 0)
                rest(p, 2)
                low_part(p, 1)
                rest(p, 3)
                max_parts(p, 1, 0)
                low_part(p, 2)
                low_part(p, 3)

            drive(pool, slot, gather, [])


_INS = ["x", "txt", "eye"] + ["L0_tok_" + n for n in ("W1", "b1", "W2", "b2")] \
    + ["L0_attn_" + n for n in ("Wq", "bq", "Wl", "bl", "Wk", "bk", "Wv", "bv", "Wo", "bo")] \
    + ["L0_ffn_" + n for n in ("Wg", "A", "B")]


def kernel(**inputs):
    import numpy as np
    import concourse.bacc as bacc
    from concourse.bass_utils import run_bass_kernel_spmd

    nc = bacc.Bacc("TRN2", target_bir_lowering=False, num_devices=1)
    arrays, args = {}, []
    inputs["eye"] = np.eye(128, dtype=np.float32)
    for name in _INS:
        a = np.ascontiguousarray(inputs[name])
        arrays[f"in_{name}"] = a
        args.append(nc.dram_tensor(f"in_{name}", a.shape, mybir.dt.from_np(a.dtype), kind="ExternalInput").ap())
    args.append(nc.dram_tensor("out_tokens", (IMAGES, TOK, D), F32, kind="ExternalOutput").ap())
    early_fusion(nc, *args)
    r = run_bass_kernel_spmd(nc, [arrays], core_ids=[0])
    return r.results[0]["out_tokens"]
```

```python
from contextlib import ExitStack

import concourse.bass as bass
from concourse import mybir

F32 = mybir.dt.float32
F32R = mybir.dt.float32r
BF16 = mybir.dt.bfloat16
I32 = mybir.dt.int32
U32 = mybir.dt.uint32
ALU = mybir.AluOpType
ACT = mybir.ActivationFunctionType
AX_X = mybir.AxisListType.X

IMAGES, CH, SIDE, PATCH = 128, 3, 224, 16
GRID = SIDE // PATCH
PATCHES = GRID * GRID
TXT = 77
TOK = PATCHES + TXT
D = 256
HEADS, HD = 16, 16
LAT = D // 4
EXPERTS, RANK = 8, 16
ER = EXPERTS * RANK
EPS = 1e-5
GROUP = 4
GROUPS = IMAGES // GROUP
ROWS = GROUP * GRID
KT1 = CH * PATCH * PATCH // 128
HALF = GRID // 2
CHUNKS = [(0, 2), (2, 2), (4, 2), (6, 1)]
QT = [98, 98, TXT]
QO = [0, 98, 196]
REST = TOK - 256
BLOCK = 32
TOKP = 256 + BLOCK
HEADS4 = HEADS // 4
TILES4 = 9
TILES = HEADS4 * TILES4
SLOTS = 6
QPART = [0, 0, 0, 1, 1, 2]
KPART = [0, 1, 2, 0, 1, 0]
SROWS = SLOTS * HD
XROWS = SROWS + 3
VW = 32
CLEARS, SETUP_V = 20, 14
LCOLS = TOK + TOK % 2
GC = EXPERTS + ER
POSITIONS = TILES
PLAN = dict(
    max_t1=(10,), weigh3=(0, 1, 2), values=(3, 4, 6), expert_t=(5,), expert_out=(7, 8, 9),
    layer2=(10, 11), tok_t=(7, 12, 22), weigh0=(14, 15, 17), out_t=(12, 13, 15), otok_t=(16, 17),
    xn1_t=(18, 19), q=(21, 23), weigh1=(19, 21, 23), latent=(20,), out_project=(20, 22, 24), k=(24, 25), max_t0=(26,),
    z0=(26, 27, 28), xn2_t=(30, 31), weigh2=(28, 29, 30), expert_in=(32, 33, 34), z1=(32, 34, 35),
    tanh=(0,), gate_exp=(35,), q_high=(22, 24), k_high=(25, 26),
    gate_weights=(0,), product=(1,), expert_weigh=(3,), stats1=(11, 12, 12), aggregate1=(13,),
    apply1=(15, 16, 17), latent_low=(21,), latent_rest=(24,), stats2=(22, 23, 25), aggregate2=(25,),
    q_mid=(24, 26), k_mid=(27, 28),
    apply2=(27, 28, 29), gate_top=(33, 34, 35), gate_choice=(35,), gate_mask=(35,))
MD_KINDS = ("max_t1", "expert_out", "layer2", "out_t", "latent", "out_project", "max_t0", "expert_in")
V_BANKS = 3
V_ORDER = sorted([(q, 0, "score", q) for q in range(POSITIONS)]
                 + [(at, 1, kind, t) for kind in MD_KINDS for t, at in enumerate(PLAN[kind])])
V_BANK = {(kind, t): n % V_BANKS for n, (_, _, kind, t) in enumerate(V_ORDER)}
MA_SLOT, MD_SLOT = 19, 17


def early_fusion(nc, x, txt, eye, W1, b1, W2, b2, Wq, bq, Wl, bl, Wk, bk, Wv, bv, Wo, bo, Wg, A, B, out):
    ctx = ExitStack()

    def sb(name, shape, dt=F32):
        return ctx.enter_context(nc.sbuf_tensor(name, shape, dt))

    def sem(name):
        return ctx.enter_context(nc.semaphore(name))

    with ctx:
        w1 = sb("w1", [128, KT1, D])
        w2 = sb("w2", [128, 2, D])
        wq = sb("wq", [128, 2, D])
        wqp = sb("wqp", [128, 2, 2, HD, 8])
        wo = sb("wo", [128, 2, D])
        wl = sb("wl", [128, 2, 2, LAT])
        wkv = sb("wkv", [128, 2, D])
        wkvh = sb("wkvh", [128, 2, D], F32R)
        wkvl = sb("wkvl", [128, 2, D], F32R)
        wga = sb("wga", [128, 2, GC])
        wb = sb("wb", [ER, D])
        wk = sb("wk", [128, D])
        blc = sb("blc", [128, 1])
        b1c = sb("b1c", [128, 2])
        bqc = sb("bqc", [128, 2])
        bkc = sb("bkc", [128, 2])
        bvc = sb("bvc", [128, 2])
        bvw = sb("bvw", [128, 2, QT[0]])
        b2r = sb("b2r", [QT[0], D])
        cor = sb("cor", [QT[0], D])
        ident = sb("ident", [128, 128])
        iota_i = sb("iota_i", [QT[0], 3, EXPERTS], I32)
        iota_e = sb("iota_e", [QT[0], 3, EXPERTS])

        raw = sb("raw", [128, CH * PATCH, HALF, PATCH])
        rawp = sb("rawp", [128, 2, CH * PATCH, PATCH])
        xT = sb("xT", [128, KT1, 2, 2, ROWS])
        zring = sb("zring", [128, 2, 2, GRID, GROUP, GRID])
        tnh = sb("tnh", [128, 2, PATCHES])
        h1 = sb("h1", [128, 2, PATCHES])
        hres = sb("hres", [QT[0], 4, 3, D])
        xn1 = sb("xn1", [QT[0], 3, D])
        xn2 = sb("xn2", [QT[0], 3, D])
        xnT1 = sb("xnT1", [128, 2, TOK])
        xnT2 = sb("xnT2", [128, 2, TOK])
        latR = sb("latR", [128, 4, BLOCK], F32R)
        latT = sb("latT", [128, TOKP], F32R)
        qkf = sb("qkf", [128, 4, TOK])
        qkr = sb("qkr", [128, 4, TOK])
        parts = sb("parts", [128, 3, 4, TOK], BF16)
        qst = sb("qst", [XROWS, 2, HEADS, TOKP], BF16)
        kst = sb("kst", [XROWS, 2, HEADS, TOKP], BF16)
        mxs = sb("mxs", [128, 4, 3, 8])
        mxd = sb("mxd", [128, 3, 8])
        mxp = sb("mxp", [128, 3, 3, 8], BF16)
        msp = sb("msp", [24, 384], BF16)
        ident_b = sb("ident_b", [128, 128], BF16)
        vaug = sb("vaug", [128, 2, 2, HEADS, VW])
        vrest = sb("vrest", [128, 2, HEADS4, 128])
        prob = sb("prob", [128, 2, TILES4, TOK])
        oT = sb("oT", [128, 4, TOK])
        orec = sb("orec", [QT[0], 3, HEADS])
        otok = sb("otok", [QT[0], 3, D])
        otT = sb("otT", [128, 2, TOK])
        st = [sb(f"st{i}", [QT[0], 3, 6]) for i in range(2)]
        mv = [sb(f"mv{i}", [QT[0], 3, 2]) for i in range(2)]
        inv = [sb(f"inv{i}", [QT[0], 2, 3]) for i in range(2)]
        minus_half = sb("minus_half", [QT[0], 3])
        ga = sb("ga", [QT[0], 3, GC])
        gev = sb("gev", [QT[0], 4, 3])
        top = sb("top", [QT[0], 3, 8])
        topi = sb("topi", [QT[0], 3, 8], U32)
        cws = sb("cws", [QT[0], 5, 3, EXPERTS])
        hw = sb("hw", [QT[0], 3, ER])
        hwT = sb("hwT", [ER, TOK])
        ost = sb("ost", [QT[0], 3, D])

        ps_v = [ctx.enter_context(nc.psum_tensor(f"ps_v{i}", [128, 512], F32)) for i in range(V_BANKS)]
        ps_st = [ctx.enter_context(nc.psum_tensor(f"ps_st{i}", [128, 512], F32)) for i in range(2)]
        ps_po = ctx.enter_context(nc.psum_tensor("ps_po", [128, 512], F32))
        ps_ma = [ctx.enter_context(nc.psum_tensor(f"ps_ma{i}", [128, 512], F32)) for i in range(2)]

        sm_full, sm_free = sem("sm_full"), sem("sm_free")
        st_full, exp_done = sem("st_full"), sem("exp_done")
        po_full, po_free = sem("po_full"), sem("po_free")
        ma_full, ma_free = sem("ma_full"), sem("ma_free")
        md_full, md_free = sem("md_full"), sem("md_free")
        w_in, b_in = sem("w_in"), sem("b_in")
        raw_in = sem("raw_in")
        rawp_done = sem("rawp_done")
        rawp_read = sem("rawp_read")
        raw_clear = sem("raw_clear")
        txt_in = sem("txt_in")
        stack_in = [sem(f"stack_in{i}") for i in range(4)]
        mrow_in = [sem(f"mrow_in{i}") for i in range(4)]
        store = sem("store")
        tanh_done, h1_done = sem("tanh_done"), sem("h1_done")
        stat = [sem("stat1"), sem("stat2")]
        eps_added = [sem("eps_added1"), sem("eps_added2")]
        rstd = [sem("rstd1"), sem("rstd2")]
        lat_high, lat_copied = sem("lat_high"), sem("lat_copied")
        xn_done = [sem("xn1_done"), sem("xn2_done")]
        const_added = sem("const_added")
        hi_done, mid_done = sem("hi_done"), sem("mid_done")
        res_done, lo_done = sem("res_done"), sem("lo_done")
        mchain, msplit = sem("mchain"), sem("msplit")
        msp_done = sem("msp_done")
        orec_done = sem("orec_done")
        top_done = sem("top_done")
        gexp_done = sem("gexp_done")
        gden_done = sem("gden_done")
        mask_done = sem("mask_done")
        gchain, cw_done = sem("gchain"), sem("cw_done")
        hw_done = sem("hw_done")
        passed = sem("passed")
        cleared, setup_pe, setup_v, setup_g = sem("cleared"), sem("setup_pe"), sem("setup_v"), sem("setup_g")

        class Linear:

            def __init__(self, turn, a, b):
                self.turn, self.a, self.b = turn, a, b

            def __add__(self, n):
                return Linear(self.turn, self.a, self.b + n)

            def __sub__(self, n):
                return Linear(self.turn, self.a, self.b - n)

            def __mul__(self, n):
                return Linear(self.turn, self.a * n, self.b * n)

            __radd__, __rmul__ = __add__, __mul__

            def value(self):
                return self.turn * self.a + self.b

        def index(v):
            return v.value() if isinstance(v, Linear) else v

        def count(v):
            assert (v.b if isinstance(v, Linear) else v) > 0
            return index(v)

        def due(v):
            return isinstance(v, Linear) or v > 0


        class Units:

            def __init__(self, banks, per_slot):
                self.banks, self.per_turn, self.count, self.g, self.start = banks, GROUP * per_slot, 0, None, 0
                self.made = 0

            def enter(self, g):
                assert self.per_turn % self.banks == 0
                self.g, self.start = g, self.count

            def leave(self, turns):
                assert self.count - self.start == self.per_turn, (self.count - self.start, self.per_turn)
                self.count, self.g = self.start + turns * self.per_turn, None

            def so_far(self, ahead=0):
                n = self.count + ahead
                return n if self.g is None else Linear(self.g, self.per_turn, n)

            def next(self):
                self.count += 1
                self.made += 1
                return (self.count - 1) % self.banks, self.so_far()

        class Slot:

            def __init__(self, g, s, tok=True):
                self.g, self.s, self.tok = g, s, tok

            def image(self, k):
                return self.g * GROUP + (2 + self.s + k)

            def place(self, k):
                return index(self.image(k))

            def mod(self, k, m):
                return (2 + self.s + k) % m

            def has(self, k):
                i = self.image(k)
                return not isinstance(i, int) or 0 <= i < IMAGES

            def group(self):
                return self.g + 2

            def landed(self, k, each):
                return (self.g * 2 + ((2 + self.s + k) // 2 + 1)) * each

        def units(kind, q):
            return [u for u, at in enumerate(PLAN[kind]) if at == q]

        TURNS = GROUPS - 2
        HEAD = [Slot(-2, s) for s in range(4)]
        FILL = [Slot(-1, s) for s in range(4)]
        DRAIN = [Slot(TURNS, s, tok=False) for s in range(4)] + [Slot(TURNS + 1, s, tok=False) for s in range(4)]

        def drive(eng, slot, tok_only, counters):
            for p in HEAD:
                tok_only(p)
            for p in FILL:
                slot(p)
            with eng.Fori(0, TURNS) as g:
                for c in counters:
                    c.enter(g)
                for s in range(4):
                    copy = eng.alloc_register(f"turn{s}")
                    eng.reg_mov(copy, g)
                    turn = eng.snap(copy, min_val=0, max_val=TURNS - 1)
                    for c in counters:
                        c.g = turn
                    slot(Slot(Linear(turn, 1, 0), s))
            for c in counters:
                c.leave(TURNS)
            for p in DRAIN:
                slot(p)

        STACK, MROW, RAW, STORE = 12 * 16, 4 * 16, 24 * 16, 3 * 16
        block = ctx.enter_context(nc.Block())

        x_v = x.rearrange("b c (gh ph) w -> b gh c ph w", ph=PATCH)
        out_v = out[:, 0:PATCHES, :].rearrange("b (gh gw) d -> b gw gh d", gw=GRID)

        @block.sync
        def _(sp):
            md = Units(1, MD_SLOT)

            def load_raw(group):
                first = group * GROUP if isinstance(group, int) else index(group) % GROUPS * GROUP
                for half in range(2):
                    for b in range(GROUP):
                        for c in range(CH):
                            row = 64 * half + b * GRID
                            sp.dma_start(raw[row:row + GRID, c * PATCH:(c + 1) * PATCH, :, :]
                                         .rearrange("p r w q -> p r (w q)"),
                                         x_v[first + b, :, c, :,
                                             half * HALF * PATCH:(half + 1) * HALF * PATCH]).then_inc(raw_in, 16)

            sp.sem_inc(store, 16)
            sp.wait_ge(raw_clear, 1)
            load_raw(0)
            sp.dma_start(ident[:], eye).then_inc(w_in, 16)
            for dst, src in ((w1, W1), (w2, W2), (wq, Wq), (wo, Wo)):
                sp.dma_start(dst[:], src.rearrange("(k p) n -> p k n", p=128)).then_inc(w_in, 16)
            for a in range(2):
                sp.dma_start(wl[:, :, a, :], Wl.rearrange("(k p) n -> p k n", p=128)).then_inc(w_in, 16)
                sp.dma_start(wk[a * LAT:(a + 1) * LAT, :], Wk).then_inc(w_in, 16)
                sp.dma_start(wkv[a * LAT:(a + 1) * LAT, 1, :], Wv).then_inc(w_in, 16)
                sp.dma_start(blc[a * LAT:(a + 1) * LAT, :], bl.rearrange("(p a) -> p a", a=1)).then_inc(b_in, 16)
            sp.dma_start(wga[:, :, 0:EXPERTS], Wg.rearrange("(k p) e -> p k e", p=128)).then_inc(w_in, 16)
            for k in range(2):
                sp.dma_start(wga[:, k, EXPERTS:GC].rearrange("p (e r) -> p e r", e=EXPERTS),
                             A[:, k * 128:(k + 1) * 128, :].rearrange("e p r -> p e r")).then_inc(w_in, 16)
            sp.dma_start(wb[:], B.rearrange("e r d -> (e r) d")).then_inc(w_in, 16)
            for dst, src in ((b1c, b1), (bvc, bv)):
                for k in range(2):
                    sp.dma_start(dst[:, k:k + 1], src[k * 128:(k + 1) * 128].rearrange("(p a) -> p a", a=1)) \
                      .then_inc(b_in, 16)
            for dst, src in ((bqc, bq), (bkc, bk)):
                for k in range(2):
                    sp.dma_start(dst[:, k:k + 1], src[k * 128:(k + 1) * 128].rearrange("(h d) -> d h", h=8),
                                 allow_slow_non_contiguous=True) \
                      .then_inc(b_in, 16)
            sp.dma_start(b2r[:], b2.rearrange("(a d) -> a d", a=1).broadcast_to([QT[0], D])).then_inc(b_in, 16)
            sp.dma_start(cor[:], bo.rearrange("(a d) -> a d", a=1).broadcast_to([QT[0], D])).then_inc(b_in, 16)
            sp.wait_ge(cleared, CLEARS)

            def reload(p):
                if p.tok and p.s == 3:
                    sp.wait_ge(rawp_done, count(4 * p.group() + 4))
                    sp.sem_inc(passed, 1)
                    load_raw(p.group() + 1)

            def text(p):
                if p.has(2):
                    if p.has(-2):
                        sp.wait_ge(md_free, count(md.so_far()))
                    sp.sem_inc(passed, 1)
                    sp.dma_start(hres[0:TXT, p.mod(2, 4), 2, :], txt[p.place(2), :, :]).then_inc(txt_in, 16)

            def max_rows(p, k, half):
                if p.has(k):
                    u, y = 2 * p.image(k) + half, p.mod(k, 2)
                    sp.wait_ge(msp_done, count(u + 1))
                    sp.sem_inc(passed, 1)
                    if due(TILES * p.image(k - 2) + TILES // 2 * (half + 1)):
                        sp.wait_ge(st_full, count(TILES * p.image(k - 2) + TILES // 2 * (half + 1)))
                    sp.sem_inc(passed, 1)
                    rows = qst[SROWS:XROWS, y, 8 * half:8 * half + 8, :]
                    sp.dma_start(rows[:, :, 0:256], msp[:, 0:256]).then_inc(mrow_in[2 * y + half], 16)
                    for r in range(3):
                        sp.dma_start(rows[r:r + 1, :, 256:TOK],
                                     msp[8 * r:8 * r + 2, 256:384].rearrange("g (j c) -> g j c", j=4)[:, :, 0:REST]) \
                          .then_inc(mrow_in[2 * y + half], 16)

            def stack(p, half, which):
                if p.has(2):
                    if which == 0 and due(TILES * p.image(0) + TILES // 2 * (half + 1)):
                        sp.wait_ge(st_full, count(TILES * p.image(0) + TILES // 2 * (half + 1)))
                        sp.sem_inc(passed, 1)
                    y, u = p.mod(2, 2), 2 * which + half
                    sp.wait_ge(hi_done, count(4 * p.image(2) + u + 1))
                    sp.wait_ge(mid_done, count(4 * p.image(2) + u + 1))
                    sp.wait_ge(lo_done, count(4 * p.image(2) + u + 1))
                    sp.sem_inc(passed, 1)
                    for row, part in enumerate((QPART, KPART)[which]):
                        sp.dma_start((qst, kst)[which][row * HD:(row + 1) * HD, y, 8 * half:8 * half + 8, 0:TOK],
                                     parts[:, part, u, :]).then_inc(stack_in[2 * y + half], 16)

            def save(p):
                if p.has(-2):
                    i = p.place(-2)
                    sp.wait_ge(md_free, count(md.so_far()))
                    sp.sem_inc(passed, 1)
                    for t in range(2):
                        sp.dma_start(out_v[i, t * HALF:(t + 1) * HALF, :, :], ost[0:QT[t], t, :]).then_inc(store, 16)
                    sp.dma_start(out[i, PATCHES:TOK, :], ost[0:TXT, 2, :]).then_inc(store, 16)

            def slot(p):
                md.count += 3 * p.has(-2)
                text(p)
                save(p)
                max_rows(p, 0, 1)
                reload(p)
                stack(p, 0, 0)
                max_rows(p, 1, 0)
                stack(p, 0, 1)
                stack(p, 1, 0)
                stack(p, 1, 1)
                md.count += 9 * p.has(-1) + 3 * p.has(2) + 1 * p.has(0) + 1 * p.has(1)

            drive(sp, slot, reload, [md])
            sp.wait_ge(raw_in, (GROUPS + 1) * RAW)
            sp.wait_ge(store, STORE * IMAGES + 16)

        @block.tensor
        def _(pe):
            ma, md, sm = Units(2, MA_SLOT), Units(1, MD_SLOT), Units(1, TILES)
            ready = {}

            pe.wait_ge(w_in, 16 * 15)
            pe.wait_ge(setup_v, 2)
            for k in range(2):
                last = nc.tensor.matmul(ps_v[0][0:QT[0], 0:D], bvw[:, k, :], wo[:, k, :],
                                        start=(k == 0), stop=(k == 1))
            last.then_inc(setup_pe, 1)
            pe.wait_ge(setup_v, SETUP_V)
            pe.wait_ge(cleared, CLEARS)

            def ma_unit():
                bank, n = ma.next()
                if due(ma.so_far(-2)):
                    pe.wait_ge(ma_free, count(ma.so_far(-2)))
                return ps_ma[bank]

            users = {}

            def v_unit(ring, kind, t):
                bank = V_BANK[kind, t]
                ring.next()
                user, made = users.get(bank, (sm, sm.made))
                before = user.so_far(made - user.made) if bank in users else 0
                if due(before):
                    if user is sm:
                        pe.wait_ge(sm_free, count(before))
                    else:
                        pe.wait_ge(md_free, count(before))
                users[bank] = ring, ring.made
                return ps_v[bank]

            def md_unit(kind, t=0):
                return v_unit(md, kind, t)

            def tok_transpose(p, u):
                if p.tok:
                    cols = CHUNKS[p.s][1]
                    pe.wait_ge(rawp_done, count(4 * p.group() + p.s + 1))
                    bank = ma_unit()
                    pe.sem_inc(passed, 1)
                    for j in range(2):
                        k = 2 * u + j
                        for w in range(cols):
                            a = (j * cols + w) * 128
                            last = nc.tensor.transpose(bank[:, a:a + 128],
                                                       rawp[:, w, 8 * k:8 * k + 8, :]
                                                       .rearrange("p r q -> p (r q)"), ident[:])
                    last.then_inc(ma_full, 1)
                    ready["xT"] = ma.so_far()

            def tok_layer1(p, m, u):
                if p.tok:
                    n = 2 * CHUNKS[p.s][1] * ROWS
                    if u == 0:
                        pe.wait_ge(ma_free, count(ready["xT"]))
                        ready["z"] = ma_unit()
                    for k in (2 * u, 2 * u + 1):
                        last = nc.tensor.matmul(ready["z"][:, 0:n], w1[:, k, m * 128:(m + 1) * 128],
                                                xT[:, k, 0:n // (2 * ROWS), :, :].rearrange("p w a n -> p (w a n)"),
                                                start=(k == 0), stop=(k == KT1 - 1))
                        if m == 0 and k == 0:
                            last.then_inc(rawp_read, 1)
                    if u == KT1 // 2 - 1:
                        last.then_inc(ma_full, 1)

            def layer2(p, t):
                if p.has(2):
                    pe.wait_ge(h1_done, count(p.image(2) + 1))
                    bank = md_unit("layer2", t)
                    for k in range(2):
                        last = nc.tensor.matmul(bank[0:QT[t], 0:D], h1[:, k, QO[t]:QO[t] + QT[t]], w2[:, k, :],
                                                start=(k == 0), stop=(k == 1))
                    last.then_inc(md_full, 1)

            def feature_major(src, f):
                bank = ma_unit()
                for t in range(3):
                    last = nc.tensor.transpose(bank[:, QO[t]:QO[t] + QT[t]],
                                               src[0:QT[t], t, f * 128:(f + 1) * 128], ident[0:QT[t], 0:QT[t]])
                last.then_inc(ma_full, 1)

            def xn_transpose(p, k, ln, src, f):
                if p.has(k):
                    pe.wait_ge(xn_done[ln], count(3 * p.image(k) + 3))
                    feature_major(src, f)
                    ready[f"xnT{ln}"] = ma.so_far()

            def project(p, m):
                if p.has(2):
                    pe.wait_ge(ma_free, count(ready["xnT0"]))
                    bank = ma_unit()
                    for k in range(2):
                        last = nc.tensor.matmul(bank[:, 0:TOK], wqp[:, k, m, :, :].rearrange("p d h -> p (d h)"),
                                                xnT1[:, k, :], start=(k == 0), stop=(k == 1))
                    last.then_inc(ma_full, 1)

            def latent(p):
                if p.has(2):
                    pe.wait_ge(ma_free, count(ready["xnT0"]))
                    bank = md_unit("latent")
                    for k in range(2):
                        last = nc.tensor.matmul(bank[:, 0:TOK], wl[:, k, :, :].rearrange("p a n -> p (a n)"),
                                                xnT1[:, k, :], start=(k == 0), stop=(k == 1))
                    last.then_inc(md_full, 1)
                    ready["latT"] = md.so_far()

            def keys(p, m):
                if p.has(2):
                    pe.wait_ge(md_free, count(ready["latT"]))
                    bank = ma_unit()
                    for w in (wkvh, wkvl):
                        last = nc.tensor.matmul(bank[:, 0:LCOLS], w[:, 0, m * 128:(m + 1) * 128], latT[:, 0:LCOLS],
                                                start=(w is wkvh), stop=(w is wkvl))
                    last.then_inc(ma_full, 1)

            def values(p, t):
                if p.has(1):
                    if t == 2:
                        pe.wait_ge(lat_copied, count(p.image(1) + 1))
                        keys_of_tile = latR[:].rearrange("p j c -> p (j c)")
                    else:
                        keys_of_tile = latT[:, t * 128:(t + 1) * 128]
                    bank = ma_unit()
                    for w in (wkvh, wkvl):
                        last = nc.tensor.matmul(bank[:, 0:D], keys_of_tile, w[:, 1, :],
                                                start=(w is wkvh), stop=(w is wkvl))
                    last.then_inc(ma_full, 1)

            def score_tile(bank, rows, moving, u, stationary):
                g, i = divmod(u, TILES4)
                if i < 8:
                    h, t = 4 * g + i // 2, i % 2
                    return nc.tensor.matmul(bank[:, 0:TOK], stationary[0:rows, h, t * 128:(t + 1) * 128],
                                            moving[0:rows, h, 0:TOK], start=True, stop=True)
                for j in range(4):
                    last = nc.tensor.matmul(bank[BLOCK * j:BLOCK * (j + 1), 0:TOK],
                                            stationary[0:rows, 4 * g + j, 256:TOKP], moving[0:rows, 4 * g + j, 0:TOK],
                                            start=True, stop=True)
                return last

            def max_scores(p, u):
                if p.has(1):
                    y = p.mod(1, 2)
                    if u % (TILES // 2) == 0:
                        pe.wait_ge(stack_in[2 * y + u // (TILES // 2)], count(p.landed(1, STACK)))
                    score_tile(v_unit(sm, "score", u), SROWS, kst[:, y, :, :], u, qst[:, y, :, :]).then_inc(sm_full, 1)

            def key_scores(p, u):
                if p.has(0):
                    y = p.mod(0, 2)
                    if u % (TILES // 2) == 0:
                        pe.wait_ge(mrow_in[2 * y + u // (TILES // 2)], count(p.landed(0, MROW)))
                    if due(TILES * p.image(0) + u - 1):
                        pe.wait_ge(exp_done, count(TILES * p.image(0) + u - 1))
                    score_tile(ps_st[u % 2], XROWS, qst[:, y, :, :], u, kst[:, y, :, :]).then_inc(st_full, 1)

            def max_transpose(p, k, half):
                if p.has(k):
                    pe.wait_ge(msplit, count(2 * p.image(k) + half + 1))
                    bank = md_unit(("max_t0", "max_t1")[half])
                    for t in range(3):
                        last = nc.tensor.transpose(bank.bitcast(BF16)[0:24, t * 128:(t + 1) * 128],
                                                   mxp[:, t, :, :].rearrange("p r h -> p (r h)"), ident_b[:])
                    last.then_inc(md_full, 1)

            def weigh(p, k, g, t):
                if p.has(k):
                    i, y = p.image(k), p.mod(k, 2)
                    if t == 0:
                        pe.wait_ge(exp_done, count(TILES * i + TILES4 * (g + 1)))
                        if due(4 * i + g):
                            pe.wait_ge(po_free, count(4 * i + g))
                    if t < 2:
                        for j in range(4):
                            nc.tensor.matmul(ps_po[VW * j:VW * (j + 1), 0:TOK], vaug[:, y, t, 4 * g + j, :],
                                             prob[:, g % 2, 2 * j + t, :], start=(t == 0), stop=False,
                                             skip_group_check=True)
                    else:
                        nc.tensor.matmul(ps_po[:, 0:TOK], vrest[:, y, g, :], prob[:, g % 2, TILES4 - 1, :],
                                         start=False, stop=True, skip_group_check=True).then_inc(po_full, 1)

            def out_transpose(p, t):
                if p.has(-1):
                    pe.wait_ge(po_free, count(4 * p.image(-1) + 4))
                    bank = md_unit("out_t", t)
                    for g in range(4):
                        last = nc.tensor.transpose(bank[0:QT[t], g * 128:(g + 1) * 128],
                                                   oT[:, g, QO[t]:QO[t] + QT[t]], ident[:])
                    last.then_inc(md_full, 1)
                    ready["otok"] = md.so_far()

            def otok_transpose(p, f):
                if p.has(-1):
                    pe.wait_ge(md_free, count(ready["otok"]))
                    feature_major(otok, f)
                    ready["otT"] = ma.so_far()

            def out_project(p, t):
                if p.has(-1):
                    pe.wait_ge(ma_free, count(ready["otT"]))
                    bank = md_unit("out_project", t)
                    for k in range(2):
                        last = nc.tensor.matmul(bank[0:QT[t], 0:D], otT[:, k, QO[t]:QO[t] + QT[t]], wo[:, k, :],
                                                start=(k == 0), stop=(k == 1))
                    last.then_inc(md_full, 1)

            def expert_in(p, t):
                if p.has(-1):
                    pe.wait_ge(ma_free, count(ready["xnT1"]))
                    bank = md_unit("expert_in", t)
                    for k in range(2):
                        last = nc.tensor.matmul(bank[0:QT[t], 0:GC], xnT2[:, k, QO[t]:QO[t] + QT[t]],
                                                wga[:, k, :], start=(k == 0), stop=(k == 1))
                    last.then_inc(md_full, 1)

            def expert_transpose(p):
                if p.has(-2):
                    pe.wait_ge(hw_done, count(p.image(-2) + 1))
                    bank = ma_unit()
                    for t in range(3):
                        last = nc.tensor.transpose(bank[:, QO[t]:QO[t] + QT[t]], hw[0:QT[t], t, :],
                                                   ident[0:QT[t], 0:QT[t]])
                    last.then_inc(ma_full, 1)
                    ready["hwT"] = ma.so_far()

            def expert_out(p, t):
                if p.has(-2):
                    pe.wait_ge(ma_free, count(ready["hwT"]))
                    bank = md_unit("expert_out", t)
                    nc.tensor.matmul(bank[0:QT[t], 0:D], hwT[:, QO[t]:QO[t] + QT[t]], wb[:],
                                     start=True, stop=True).then_inc(md_full, 1)

            def slot(p):
                for q in range(POSITIONS):
                    max_scores(p, q)
                    key_scores(p, q)
                    for _ in units("max_t1", q):
                        max_transpose(p, 0, 1)
                    for t in units("weigh3", q):
                        weigh(p, -1, 3, t)
                    for t in units("values", q):
                        values(p, t)
                    for _ in units("expert_t", q):
                        expert_transpose(p)
                    for t in units("expert_out", q):
                        expert_out(p, t)
                    for t in units("layer2", q):
                        layer2(p, t)
                    for u in units("tok_t", q):
                        tok_transpose(p, u)
                    for t in units("weigh0", q):
                        weigh(p, 0, 0, t)
                    for t in units("out_t", q):
                        out_transpose(p, t)
                    for f in units("otok_t", q):
                        otok_transpose(p, f)
                    for f in units("xn1_t", q):
                        xn_transpose(p, 2, 0, xn1, f)
                    for m in units("q", q):
                        project(p, m)
                    for t in units("weigh1", q):
                        weigh(p, 0, 1, t)
                    for t in units("out_project", q):
                        out_project(p, t)
                    for _ in units("latent", q):
                        latent(p)
                    for m in units("k", q):
                        keys(p, m)
                    for _ in units("max_t0", q):
                        max_transpose(p, 1, 0)
                    for u in units("z0", q):
                        tok_layer1(p, 0, u)
                    for f in units("xn2_t", q):
                        xn_transpose(p, -1, 1, xn2, f)
                    for t in units("weigh2", q):
                        weigh(p, 0, 2, t)
                    for t in units("expert_in", q):
                        expert_in(p, t)
                    for u in units("z1", q):
                        tok_layer1(p, 1, u)

            def tok_only(p):
                for u in range(KT1 // 2):
                    tok_transpose(p, u)
                for m in range(2):
                    for u in range(KT1 // 2):
                        tok_layer1(p, m, u)

            drive(pe, slot, tok_only, [ma, md, sm])

        @block.scalar
        def _(act):
            ma = Units(2, MA_SLOT)
            ready = {}

            def ma_unit():
                bank, n = ma.next()
                act.wait_ge(ma_full, count(n))
                return ps_ma[bank]

            act.wait_ge(setup_v, SETUP_V)
            act.wait_ge(cleared, CLEARS)

            def tok_evac(p, u):
                if p.tok:
                    cols = CHUNKS[p.s][1]
                    bank = ma_unit()
                    nc.scalar.activation(xT[:, 2 * u:2 * u + 2, 0:cols, :, :].rearrange("p j w a n -> p (j w) a n"),
                                         bank[:, 0:2 * cols * 128].rearrange("p (t a n) -> p t a n", a=2, n=64)
                                         [:, :, :, 0:ROWS], ACT.Copy).then_inc(ma_free, 1)

            def z_evac(p, m):
                if p.tok:
                    col, cols = CHUNKS[p.s]
                    if m == 0 and p.s == 0:
                        if due((p.group() - 1) * GROUP):
                            act.wait_ge(h1_done, count((p.group() - 1) * GROUP))
                    bank = ma_unit()
                    nc.scalar.activation(zring[:, index(p.group()) % 2, m, :, :, :].rearrange("p (a w) b g -> p w a (b g)", a=2)
                                         [:, col:col + cols, :, :],
                                         bank[:, 0:2 * cols * ROWS].rearrange("p (w a n) -> p w a n", a=2, w=cols),
                                         ACT.Identity, bias=b1c[:, m:m + 1]).then_inc(ma_free, 1)

            def tanh(p):
                if p.has(2):
                    act.wait_ge(ma_free, count(ma.so_far()))
                    if due(p.image(1) + 1):
                        act.wait_ge(h1_done, count(p.image(1) + 1))
                    z = zring[:, index(p.group() - 1) % 2, :, :, p.s, :]
                    nc.scalar.activation(tnh[:].rearrange("p m (w g) -> p m w g", w=GRID), z, ACT.Tanh,
                                         scale=0.5).then_inc(tanh_done, 1)

            def value_evac(p, t):
                if p.has(1):
                    y = p.mod(1, 2)
                    bank = ma_unit()
                    if t < 2:
                        nc.scalar.activation(vaug[:, y, t, :, 0:HD],
                                             bank[:, 0:D].rearrange("p (h d) -> p h d", h=HEADS),
                                             ACT.Copy).then_inc(ma_free, 1)
                    else:
                        for j in range(4):
                            block = slice(BLOCK * j, BLOCK * (j + 1))
                            last = nc.scalar.activation(
                                vrest[block, y, :, VW * j:VW * j + HD],
                                bank[block, 0:D].rearrange("p (g j d) -> p g j d", g=HEADS4, j=4)[:, :, j, :], ACT.Copy)
                        last.then_inc(ma_free, 1)

            def feature_evac(p, k, dst, f):
                if p.has(k):
                    bank = ma_unit()
                    nc.scalar.activation(dst[:, f, :], bank[:, 0:TOK], ACT.Copy).then_inc(ma_free, 1)

            def qk_evac(p, u, bias):
                if p.has(2):
                    i = p.image(2)
                    if u == 0 and due(4 * i):
                        act.wait_ge(res_done, count(4 * i))
                        act.wait_ge(lo_done, count(4 * i))
                    bank = ma_unit()
                    nc.scalar.activation(qkf[:, u, :], bank[:, 0:TOK], ACT.Identity,
                                         bias=bias[:, u % 2:u % 2 + 1]).then_inc(ma_free, 1)
                    ready["qk", u] = ma.so_far()

            def high_part(p, u):
                if p.has(2):
                    if u == 0 and due(p.image(2)):
                        for half in range(2):
                            act.wait_ge(stack_in[2 * p.mod(1, 2) + half], count(p.landed(1, STACK)))
                    act.wait_ge(ma_free, count(ready["qk", u]))
                    nc.scalar.activation(parts[:, 0, u, :], qkf[:, u, :], ACT.Copy).then_inc(hi_done, 1)

            def expscore(p, u):
                if p.has(0):
                    i, (g, tile) = p.image(0), divmod(u, TILES4)
                    if tile == 0 and due(4 * i + g - 1):
                        act.wait_ge(po_full, count(4 * i + g - 1))
                    act.wait_ge(st_full, count(TILES * i + u + 1))
                    nc.scalar.activation(prob[:, g % 2, tile, :], ps_st[u % 2][:, 0:TOK], ACT.Exp,
                                         scale=HD ** -0.5).then_inc(exp_done, 1)

            def out_evac(p, k, g):
                if p.has(k):
                    act.wait_ge(po_full, count(4 * p.image(k) + g + 1))
                    nc.scalar.activation(oT[:, g, :], ps_po[:, 0:TOK], ACT.Copy).then_inc(po_free, 1)

            def gate_exp(p):
                if p.has(-1):
                    i = p.image(-1)
                    act.wait_ge(top_done, count(7 * i + 4))
                    if due(i):
                        act.wait_ge(cw_done, count(i))
                    nc.scalar.activation(gev[:, 1, :], gev[:, 0, :], ACT.Exp).then_inc(gexp_done, 1)

            def expert_evac(p):
                if p.has(-2):
                    bank = ma_unit()
                    nc.scalar.activation(hwT[:, :], bank[:, 0:TOK], ACT.Copy).then_inc(ma_free, 1)

            def slot(p):
                for q in range(POSITIONS):
                    expscore(p, q)
                    for _ in units("tanh", q):
                        tanh(p)
                    if q == PLAN["weigh3"][2]:
                        out_evac(p, -1, 3)
                    for t in units("values", q):
                        value_evac(p, t)
                    for _ in units("expert_t", q):
                        expert_evac(p)
                    for u in units("tok_t", q):
                        tok_evac(p, u)
                    if q == PLAN["weigh0"][2]:
                        out_evac(p, 0, 0)
                    for f in units("otok_t", q):
                        feature_evac(p, -1, otT, f)
                    for f in units("xn1_t", q):
                        feature_evac(p, 2, xnT1, f)
                    for m in units("q", q):
                        qk_evac(p, m, bqc)
                    for m in units("q_high", q):
                        high_part(p, m)
                    if q == PLAN["weigh1"][2]:
                        out_evac(p, 0, 1)
                    for m in units("k", q):
                        qk_evac(p, 2 + m, bkc)
                    for m in units("k_high", q):
                        high_part(p, 2 + m)
                    if q == PLAN["z0"][2]:
                        z_evac(p, 0)
                    for f in units("xn2_t", q):
                        feature_evac(p, -1, xnT2, f)
                    if q == PLAN["weigh2"][2]:
                        out_evac(p, 0, 2)
                    if q == PLAN["z1"][2]:
                        z_evac(p, 1)
                    for _ in units("gate_exp", q):
                        gate_exp(p)

            def tok_only(p):
                for u in range(KT1 // 2):
                    tok_evac(p, u)
                z_evac(p, 0)
                z_evac(p, 1)

            drive(act, slot, tok_only, [ma])

        @block.vector
        def _(dve):
            md = Units(1, MD_SLOT)
            ready = {}

            def md_unit(kind, t=0):
                _, n = md.next()
                dve.wait_ge(md_full, count(n))
                return ps_v[V_BANK[kind, t]]

            nc.vector.memset(raw[:], 0.0).then_inc(raw_clear, 1)
            for c in range(2):
                nc.vector.memset(mv[c][:], 0.0).then_inc(cleared, 1)
            nc.vector.memset(hres[:], 0.0).then_inc(cleared, 1)
            nc.vector.memset(ga[:], 0.0).then_inc(cleared, 1)
            nc.vector.memset(top[:], 0.0).then_inc(cleared, 1)
            nc.vector.memset(topi[:], 0).then_inc(cleared, 1)
            nc.vector.memset(minus_half[:], -0.5).then_inc(cleared, 1)
            nc.vector.memset(vaug[:], 0.0).then_inc(cleared, 1)
            nc.vector.memset(vrest[:], 0.0).then_inc(cleared, 1)
            nc.vector.memset(mxs[:], 0.0).then_inc(cleared, 1)
            nc.vector.memset(kst[SROWS:XROWS, :, :, 0:TOK], 1.0).then_inc(cleared, 1)
            for stack in (qst, kst):
                nc.vector.memset(stack[:, :, :, TOK:TOKP], 0.0).then_inc(cleared, 1)
            nc.vector.memset(wkvl[LAT:128, :, :].bitcast(F32), 0.0).then_inc(cleared, 1)
            nc.vector.memset(latT[:].bitcast(F32), 0.0).then_inc(cleared, 1)
            dve.wait_ge(cleared, CLEARS - 5)
            nc.vector.memset(vaug[:, :, :, :, HD:HD + 1], 1.0).then_inc(cleared, 1)
            for j in range(4):
                nc.vector.memset(vrest[BLOCK * j:BLOCK * j + REST, :, :, VW * j + HD:VW * j + HD + 1], 1.0) \
                  .then_inc(cleared, 1)

            dve.wait_ge(w_in, 16 * 15)
            dve.wait_ge(b_in, 16 * 12)
            for k in range(2):
                nc.vector.tensor_copy(bvw[:, k, :], bvc[:, k:k + 1].broadcast_to([128, QT[0]])).then_inc(setup_v, 1)
            for m in range(2):
                nc.vector.tensor_copy(wkv[:, 0, m * 128:(m + 1) * 128].rearrange("p (d h) -> p d h", h=8),
                                      wk[:, m * 128:(m + 1) * 128].rearrange("p (h d) -> p d h", h=8)) \
                  .then_inc(setup_v, 1)
                for k in range(2):
                    nc.vector.tensor_copy(wqp[:, k, m, :, :], wq[:, k, m * 128:(m + 1) * 128]
                                          .rearrange("p (h d) -> p d h", h=8)).then_inc(setup_v, 1)
            nc.vector.tensor_scalar(w2[:], w2[:], 0.5, None, ALU.mult).then_inc(setup_v, 1)
            dve.wait_ge(setup_g, 1)
            nc.vector.tensor_copy(iota_e[:], iota_i[:]).then_inc(setup_v, 1)
            nc.vector.tensor_copy(ident_b[:], ident[:]).then_inc(setup_v, 1)
            dve.wait_ge(setup_v, 11)
            nc.vector.tensor_copy(wkvh[:], wkv[:]).then_inc(setup_v, 1)
            dve.wait_ge(setup_v, 12)
            nc.vector.tensor_tensor(wkvl[0:LAT, :, :], wkv[0:LAT, :, :], wkvh[0:LAT, :, :], ALU.subtract) \
              .then_inc(setup_v, 1)
            dve.wait_ge(setup_pe, 1)
            nc.vector.tensor_tensor(cor[:], cor[:], ps_v[0][0:QT[0], 0:D], ALU.add).then_inc(setup_v, 1)

            def product(p):
                if p.has(2):
                    dve.wait_ge(tanh_done, count(p.image(2) + 1))
                    z = zring[:, index(p.group() - 1) % 2, :, :, p.s, :].rearrange("p m w g -> p (m w) g")
                    nc.vector.scalar_tensor_tensor(h1[:].rearrange("p m (w g) -> p (m w) g", w=GRID),
                                                   tnh[:].rearrange("p m (w g) -> p (m w) g", w=GRID), 1.0, z,
                                                   ALU.add, ALU.mult).then_inc(h1_done, 1)

            def reduce_max(p, u):
                if p.has(1):
                    y, (g, tile) = p.mod(1, 2), divmod(u, TILES4)
                    dst = mxs[:, 2 * y + g // 2, 2, g % 2:g % 2 + 1]
                    if tile < 8:
                        h = (4 * g + tile // 2) % 8
                        dst = mxs[:, 2 * y + g // 2, tile % 2, h:h + 1]
                    dve.wait_ge(sm_full, count(TILES * p.image(1) + u + 1))
                    nc.vector.tensor_reduce(dst, ps_v[V_BANK["score", u]][:, 0:TOK], AX_X, ALU.max, negate=True) \
                      .then_inc(sm_free, 1)

            def max_evac(p, k, half):
                if p.has(k):
                    u = 2 * p.image(k) + half
                    if due(u):
                        kk, hh = (k, 0) if half else (k - 1, 1)
                        dve.wait_ge(mrow_in[2 * p.mod(kk, 2) + hh], count(p.landed(kk, MROW)))
                    bank = md_unit(("max_t0", "max_t1")[half])
                    nc.vector.tensor_copy(msp[:], bank.bitcast(BF16)[0:24, 0:384]).then_inc(md_free, 1)
                    dve.wait_ge(md_free, count(md.so_far()))
                    dve.sem_inc(msp_done, 1)

            def normalise(p, t):
                if p.has(-1):
                    bank = md_unit("out_t", t)
                    v = bank[0:QT[t], :].rearrange("p (h w) -> p h w", h=HEADS)
                    nc.vector.reciprocal(orec[0:QT[t], t, :], v[:, :, HD:HD + 1].rearrange("p h w -> p (h w)")) \
                      .then_inc(orec_done, 1)
                    dve.wait_ge(orec_done, count(3 * p.image(-1) + t + 1))
                    nc.vector.tensor_tensor(otok[0:QT[t], t, :].rearrange("p (h d) -> p h d", h=HEADS),
                                            v[:, :, 0:HD],
                                            orec[0:QT[t], t, :].unsqueeze(2).broadcast_to([QT[t], HEADS, HD]),
                                            ALU.mult).then_inc(md_free, 1)

            def statistics(p, k, ln, t):
                if p.has(k):
                    if ln == 0 and t == 2:
                        dve.wait_ge(txt_in, count(16 * p.image(k) + 16))
                    else:
                        dve.wait_ge(md_free, count(ready["hres", t]))
                    nc.vector.bn_stats(st[ln][0:QT[t], t, :], hres[0:QT[t], p.mod(k, 4), t, :]).then_inc(stat[ln], 1)

            def aggregate(p, k, ln):
                if p.has(k):
                    for t in range(3):
                        dve.wait_ge(stat[ln], count(6 * p.image(k) + t + 1))
                        dve.sem_inc(passed, 1)
                        nc.vector.bn_aggr(mv[ln][0:QT[t], t, :], st[ln][0:QT[t], t, :]).then_inc(stat[ln], 1)

            def layer2_evac(p, t):
                if p.has(2):
                    bank = md_unit("layer2", t)
                    nc.vector.tensor_tensor(hres[0:QT[t], p.mod(2, 4), t, :], bank[0:QT[t], 0:D], b2r[0:QT[t], :],
                                            ALU.add).then_inc(md_free, 1)
                    ready["hres", t] = md.so_far()

            def latent_high(p):
                if p.has(2):
                    bank = md_unit("latent")
                    nc.vector.tensor_scalar(latT[:, 0:TOK], bank[:, 0:TOK], blc[:], None, ALU.add).then_inc(lat_high, 1)

            def latent_low(p):
                if p.has(2):
                    dve.wait_ge(lat_high, count(p.image(2) + 1))
                    low = latT[LAT:128, 0:TOK]
                    nc.vector.scalar_tensor_tensor(low, ps_v[V_BANK["latent", 0]][LAT:128, 0:TOK], blc[LAT:128, :], low, ALU.add,
                                                   ALU.subtract).then_inc(md_free, 1)
                    ready["latT"] = md.so_far()

            def latent_rest(p):
                if p.has(2):
                    dve.wait_ge(md_free, count(ready["latT"]))
                    nc.vector.tensor_copy(latR[:], latT[:, 256:TOKP].unsqueeze(1).broadcast_to([128, 4, BLOCK])) \
                      .then_inc(lat_copied, 1)

            def residual(p, t):
                if p.has(-1):
                    dve.wait_ge(const_added, count(p.image(-1) + 1))
                    bank = md_unit("out_project", t)
                    r = hres[0:QT[t], p.mod(-1, 4), t, :]
                    nc.vector.tensor_tensor(r, bank[0:QT[t], 0:D], r, ALU.add).then_inc(md_free, 1)
                    ready["hres", t] = md.so_far()

            def apply(p, k, ln, dst, t):
                if p.has(k):
                    if t == 0:
                        dve.wait_ge(rstd[ln], count(p.image(k) + 1))
                    nc.vector.tensor_scalar(dst[0:QT[t], t, :], hres[0:QT[t], p.mod(k, 4), t, :],
                                            mv[ln][0:QT[t], t, 0:1], inv[ln][0:QT[t], 1, t:t + 1],
                                            ALU.subtract, ALU.mult).then_inc(xn_done[ln], 1)

            def mid_part(p, u):
                if p.has(2):
                    dve.wait_ge(res_done, count(4 * p.image(2) + u + 1))
                    nc.vector.tensor_copy(parts[:, 1, u, :], qkr[:, u, :]).then_inc(mid_done, 1)

            def gates(p, t):
                if p.has(-1):
                    bank = md_unit("expert_in", t)
                    nc.vector.tensor_copy(ga[0:QT[t], t, :], bank[0:QT[t], 0:GC]).then_inc(md_free, 1)
                    ready["ga", t] = md.so_far()

            def gate_top(p, t):
                if p.has(-1):
                    if due(p.image(-1)):
                        dve.wait_ge(cw_done, count(p.image(-1)))
                    dve.wait_ge(md_free, count(ready["ga", t]))
                    dve.sem_inc(passed, 1)
                    nc.vector.max(top[0:QT[t], t, :], ga[0:QT[t], t, 0:EXPERTS]).then_inc(top_done, 1)

            def gate_choice(p):
                if p.has(-1):
                    i = p.image(-1)
                    dve.wait_ge(top_done, count(7 * i + 3))
                    nc.vector.tensor_tensor(gev[:, 0, :], top[:, :, 1], top[:, :, 0], ALU.subtract).then_inc(top_done, 1)
                    for t in range(3):
                        nc.vector.max_index(topi[0:QT[t], t, :], top[0:QT[t], t, :], ga[0:QT[t], t, 0:EXPERTS]) \
                          .then_inc(top_done, 1)

            def gate_mask(p):
                if p.has(-1):
                    i = p.image(-1)
                    dve.wait_ge(top_done, count(7 * i + 7))
                    for j in range(2):
                        nc.vector.tensor_tensor(cws[:, j, :, :], iota_e[:],
                                                topi[:, :, j:j + 1].broadcast_to([QT[0], 3, EXPERTS]),
                                                ALU.is_equal).then_inc(mask_done, 1)

            def gate_weights(p):
                if p.has(-2):
                    i = p.image(-2)
                    dve.wait_ge(gexp_done, count(i + 1))
                    nc.vector.tensor_scalar(gev[:, 2, :], gev[:, 1, :], 1.0, None, ALU.add).then_inc(gden_done, 1)
                    dve.wait_ge(gden_done, count(2 * i + 1))
                    nc.vector.reciprocal(gev[:, 3, :], gev[:, 2, :]).then_inc(gden_done, 1)

            def expert_weigh(p):
                if p.has(-2):
                    dve.wait_ge(cw_done, count(p.image(-2) + 1))
                    nc.vector.tensor_tensor(hw[:].rearrange("p t (e r) -> p t e r", e=EXPERTS),
                                            ga[:, :, EXPERTS:GC].rearrange("p t (e r) -> p t e r", e=EXPERTS),
                                            cws[:, 4, :, :].unsqueeze(3).broadcast_to([QT[0], 3, EXPERTS, RANK]),
                                            ALU.mult).then_inc(hw_done, 1)

            def final(p, t):
                if p.has(-2):
                    if t == 0:
                        dve.wait_ge(store, count(STORE * p.image(-2) + 16))
                    bank = md_unit("expert_out", t)
                    nc.vector.tensor_tensor(ost[0:QT[t], t, :], bank[0:QT[t], 0:D],
                                            hres[0:QT[t], p.mod(-2, 4), t, :], ALU.add).then_inc(md_free, 1)

            def slot(p):
                for q in range(POSITIONS):
                    reduce_max(p, q)
                    for _ in units("gate_weights", q):
                        gate_weights(p)
                    for _ in units("product", q):
                        product(p)
                    for _ in units("max_t1", q):
                        max_evac(p, 0, 1)
                    for _ in units("expert_weigh", q):
                        expert_weigh(p)
                    for t in units("expert_out", q):
                        final(p, t)
                    for t in units("layer2", q):
                        layer2_evac(p, t)
                    for t in units("stats1", q):
                        statistics(p, 2, 0, t)
                    for _ in units("aggregate1", q):
                        aggregate(p, 2, 0)
                    for t in units("out_t", q):
                        normalise(p, t)
                    for t in units("apply1", q):
                        apply(p, 2, 0, xn1, t)
                    for t in units("out_project", q):
                        residual(p, t)
                    for t in units("stats2", q):
                        statistics(p, -1, 1, t)
                    for _ in units("aggregate2", q):
                        aggregate(p, -1, 1)
                    for m in units("q_mid", q):
                        mid_part(p, m)
                    for m in units("k_mid", q):
                        mid_part(p, 2 + m)
                    for _ in units("latent", q):
                        latent_high(p)
                    for _ in units("latent_low", q):
                        latent_low(p)
                    for _ in units("latent_rest", q):
                        latent_rest(p)
                    for _ in units("max_t0", q):
                        max_evac(p, 1, 0)
                    for t in units("apply2", q):
                        apply(p, -1, 1, xn2, t)
                    for t in units("expert_in", q):
                        gates(p, t)
                    for t in units("gate_top", q):
                        gate_top(p, t)
                    for _ in units("gate_choice", q):
                        gate_choice(p)
                    for _ in units("gate_mask", q):
                        gate_mask(p)

            drive(dve, slot, lambda p: None, [md])

        @block.gpsimd
        def _(pool):
            nc.gpsimd.iota(iota_i[:], pattern=[[0, 3], [1, EXPERTS]], base=0, channel_multiplier=0).then_inc(setup_g, 1)
            pool.wait_ge(setup_v, SETUP_V)
            pool.wait_ge(cleared, CLEARS)

            def gather(p):
                if p.tok:
                    col, cols = CHUNKS[p.s]
                    u = 4 * p.group() + p.s
                    pool.wait_ge(raw_in, count((p.group() + 1) * RAW))
                    if due(u):
                        pool.wait_ge(rawp_read, count(u))
                    pool.sem_inc(passed, 1)
                    nc.gpsimd.tensor_scalar(rawp[:, 0:cols, :, :],
                                            raw[:, :, col:col + cols, :].rearrange("p r w q -> p w r q"), 1.0, 1.0,
                                            ALU.mult, ALU.mult).then_inc(rawp_done, 1)

            def rsqrt(p, k, ln):
                if p.has(k):
                    i = p.image(k)
                    pool.wait_ge(stat[ln], count(6 * i + 6))
                    if due(3 * i):
                        pool.wait_ge(xn_done[ln], count(3 * i))
                    pool.sem_inc(passed, 1)
                    nc.gpsimd.tensor_scalar(inv[ln][:, 0, :], mv[ln][:, :, 1], EPS, 1.0, ALU.add, ALU.mult) \
                      .then_inc(eps_added[ln], 1)
                    pool.wait_ge(eps_added[ln], count(i + 1))
                    nc.gpsimd.tensor_tensor(inv[ln][:, 1, :], inv[ln][:, 0, :], minus_half[:], ALU.pow) \
                      .then_inc(rstd[ln], 1)

            def add_constant(p):
                if p.has(2):
                    i = p.image(2)
                    pool.wait_ge(xn_done[0], count(3 * i + 3))
                    r = hres[:, p.mod(2, 4), :, :]
                    nc.gpsimd.tensor_tensor(r, r, cor[:].unsqueeze(1).broadcast_to([QT[0], 3, D]), ALU.add) \
                      .then_inc(const_added, 1)

            def max_parts(p, k, half):
                if p.has(k):
                    u = 2 * p.image(k) + half
                    m = mxs[:, 2 * p.mod(k, 2) + half, :, :]
                    pool.wait_ge(sm_free, count(TILES * p.image(k) + TILES // 2 * (half + 1)))
                    if due(u):
                        pool.wait_ge(msp_done, count(u))
                    pool.sem_inc(passed, 1)
                    nc.gpsimd.tensor_scalar(mxp[:, :, 0, :], m, 1.0, 1.0, ALU.mult, ALU.mult).then_inc(mchain, 1)
                    pool.wait_ge(mchain, count(3 * u + 1))
                    nc.gpsimd.tensor_tensor(mxd[:], m, mxp[:, :, 0, :], ALU.subtract).then_inc(mchain, 1)
                    pool.wait_ge(mchain, count(3 * u + 2))
                    pool.sem_inc(passed, 1)
                    nc.gpsimd.tensor_scalar(mxp[:, :, 1, :], mxd[:], 1.0, 1.0, ALU.mult, ALU.mult).then_inc(mchain, 1)
                    pool.wait_ge(mchain, count(3 * u + 3))
                    nc.gpsimd.tensor_tensor(mxp[:, :, 2, :], mxd[:], mxp[:, :, 1, :], ALU.subtract).then_inc(msplit, 1)

            def rest(p, u):
                if p.has(2):
                    pool.wait_ge(hi_done, count(4 * p.image(2) + u + 1))
                    nc.gpsimd.tensor_tensor(qkr[:, u, :], qkf[:, u, :], parts[:, 0, u, :],
                                            ALU.subtract).then_inc(res_done, 1)

            def low_part(p, u):
                if p.has(2):
                    pool.wait_ge(mid_done, count(4 * p.image(2) + u + 1))
                    nc.gpsimd.tensor_tensor(parts[:, 2, u, :], qkr[:, u, :], parts[:, 1, u, :],
                                            ALU.subtract).then_inc(lo_done, 1)

            def combine(p):
                if p.has(-2):
                    i = p.image(-2)
                    pool.wait_ge(gden_done, count(2 * i + 2))
                    pool.wait_ge(mask_done, count(2 * i + 2))
                    nc.gpsimd.tensor_tensor(gev[:, 2, :], gev[:, 1, :], gev[:, 3, :], ALU.mult).then_inc(gchain, 1)
                    pool.wait_ge(gchain, count(3 * i + 1))
                    for j, w in ((0, 3), (1, 2)):
                        nc.gpsimd.tensor_tensor(cws[:, 2 + j, :, :], cws[:, j, :, :],
                                                gev[:, w, :].unsqueeze(2).broadcast_to([QT[0], 3, EXPERTS]),
                                                ALU.mult).then_inc(gchain, 1)
                    pool.wait_ge(gchain, count(3 * i + 3))
                    nc.gpsimd.tensor_tensor(cws[:, 4, :, :], cws[:, 2, :, :], cws[:, 3, :, :], ALU.add) \
                      .then_inc(cw_done, 1)

            def slot(p):
                combine(p)
                max_parts(p, 0, 1)
                gather(p)
                rsqrt(p, 2, 0)
                add_constant(p)
                rest(p, 0)
                rest(p, 1)
                low_part(p, 0)
                max_parts(p, 1, 0)
                low_part(p, 1)
                rest(p, 2)
                rest(p, 3)
                rsqrt(p, -1, 1)
                low_part(p, 2)
                low_part(p, 3)

            drive(pool, slot, gather, [])


_INS = ["x", "txt", "eye"] + ["L0_tok_" + n for n in ("W1", "b1", "W2", "b2")] \
    + ["L0_attn_" + n for n in ("Wq", "bq", "Wl", "bl", "Wk", "bk", "Wv", "bv", "Wo", "bo")] \
    + ["L0_ffn_" + n for n in ("Wg", "A", "B")]


def kernel(**inputs):
    import numpy as np
    import concourse.bacc as bacc
    from concourse.bass_utils import run_bass_kernel_spmd

    nc = bacc.Bacc("TRN2", target_bir_lowering=False, num_devices=1)
    arrays, args = {}, []
    inputs["eye"] = np.eye(128, dtype=np.float32)
    for name in _INS:
        a = np.ascontiguousarray(inputs[name])
        arrays[f"in_{name}"] = a
        args.append(nc.dram_tensor(f"in_{name}", a.shape, mybir.dt.from_np(a.dtype), kind="ExternalInput").ap())
    args.append(nc.dram_tensor("out_tokens", (IMAGES, TOK, D), F32, kind="ExternalOutput").ap())
    early_fusion(nc, *args)
    r = run_bass_kernel_spmd(nc, [arrays], core_ids=[0])
    return r.results[0]["out_tokens"]
```
